# Optimizing a Trainium2 kernel written in Bass

```python
import numpy as np
import jax
import jax.numpy as jnp

def _softmax(x, axis=-1):
    return jax.nn.softmax(x, axis=axis)
def _gelu(x):
    return jax.nn.gelu(x, approximate=True)
def _silu(x):
    return jax.nn.silu(x)
def _sigmoid(x):
    return jax.nn.sigmoid(x)
def _layernorm(x, axis=-1, eps=1e-5):
    m = jnp.mean(x, axis=axis, keepdims=True)
    v = jnp.var(x, axis=axis, keepdims=True)
    return (x - m) / jnp.sqrt(v + eps)
def _scatter_add(tgt, idx, src, axis=0):
    return tgt.at[idx].add(src)
def _segment_sum(src, seg, n):
    return jax.ops.segment_sum(src, seg, n)

kernel_name = 'mk_conv_seq_d1_conv_nchw64_fd24cd'

def setup_inputs(seed: int = 0):
    np.random.seed(seed)
    _w = jnp.asarray
    def _rec_inputs():
        import jax
        import jax.numpy as jnp
        _gk = jax.random.key(seed)
        x = -7.109e-05 + 0.9999 * jax.random.normal(jax.random.fold_in(_gk, 1), (16, 64, 256, 256), jnp.float32)
        return x
    x = _rec_inputs()
    def _L0_conv_setup():
        import jax, jax.numpy as jnp
        import numpy as np
        C = 64
        RED = 16

        def _dwconv(x, w, b, pad):
            y = jax.lax.conv_general_dilated(x, w, window_strides=(1, 1), padding=[(pad, pad), (pad, pad)], dimension_numbers=('NCHW', 'OIHW', 'NCHW'), feature_group_count=x.shape[1])
            return y + b[None, :, None, None]
        key = jax.random.key(seed)
        ks = jax.random.split(key, 12)
        N, H, W = (16, 256, 256)
        s = 0.05
        return {'x': jax.random.normal(ks[0], (N, C, H, W), jnp.float32), 'w7': jax.random.normal(ks[1], (C, 1, 7, 7), jnp.float32) * s, 'b7': jax.random.normal(ks[2], (C,), jnp.float32) * s, 'w5': jax.random.normal(ks[3], (C, 1, 5, 5), jnp.float32) * s, 'b5': jax.random.normal(ks[4], (C,), jnp.float32) * s, 'w3': jax.random.normal(ks[5], (C, 1, 3, 3), jnp.float32) * s, 'b3': jax.random.normal(ks[6], (C,), jnp.float32) * s, 'fc1_w': jax.random.normal(ks[7], (C // RED, C), jnp.float32) * s, 'fc1_b': jax.random.normal(ks[8], (C // RED,), jnp.float32) * s, 'fc2_w': jax.random.normal(ks[9], (C, C // RED), jnp.float32) * s, 'fc2_b': jax.random.normal(ks[10], (C,), jnp.float32) * s, 'w1x1': jax.random.normal(ks[11], (C, C, 1, 1), jnp.float32) * s, 'b1x1': jnp.zeros((C,), jnp.float32)}
    _L0_conv_all = _L0_conv_setup()
    _L0_conv_in = {k: v for k, v in _L0_conv_all.items() if k in ('w7', 'b7', 'w5', 'b5', 'w3', 'b3', 'fc1_w', 'fc1_b', 'fc2_w', 'fc2_b', 'w1x1', 'b1x1', )}
    del _L0_conv_all

    return {
        "x": x,
        "L0_conv_w7": _L0_conv_in["w7"],
        "L0_conv_b7": _L0_conv_in["b7"],
        "L0_conv_w5": _L0_conv_in["w5"],
        "L0_conv_b5": _L0_conv_in["b5"],
        "L0_conv_w3": _L0_conv_in["w3"],
        "L0_conv_b3": _L0_conv_in["b3"],
        "L0_conv_fc1_w": _L0_conv_in["fc1_w"],
        "L0_conv_fc1_b": _L0_conv_in["fc1_b"],
        "L0_conv_fc2_w": _L0_conv_in["fc2_w"],
        "L0_conv_fc2_b": _L0_conv_in["fc2_b"],
        "L0_conv_w1x1": _L0_conv_in["w1x1"],
        "L0_conv_b1x1": _L0_conv_in["b1x1"],
    }

def reference(x, L0_conv_w7, L0_conv_b7, L0_conv_w5, L0_conv_b5, L0_conv_w3, L0_conv_b3, L0_conv_fc1_w, L0_conv_fc1_b, L0_conv_fc2_w, L0_conv_fc2_b, L0_conv_w1x1, L0_conv_b1x1):
    import jax
    import jax.numpy as jnp
    def _L0_conv_ref(x, w7, b7, w5, b5, w3, b3, fc1_w, fc1_b, fc2_w, fc2_b, w1x1, b1x1):
        import jax, jax.numpy as jnp
        import numpy as np
        C = 64
        RED = 16

        def _dwconv(x, w, b, pad):
            y = jax.lax.conv_general_dilated(x, w, window_strides=(1, 1), padding=[(pad, pad), (pad, pad)], dimension_numbers=('NCHW', 'OIHW', 'NCHW'), feature_group_count=x.shape[1])
            return y + b[None, :, None, None]
        xm = _dwconv(x, w7, b7, 3) + _dwconv(x, w5, b5, 2) + _dwconv(x, w3, b3, 1)
        y = jnp.mean(xm, axis=(2, 3))
        y = jax.nn.relu(y @ fc1_w.T + fc1_b)
        y = jax.nn.sigmoid(y @ fc2_w.T + fc2_b)
        x_se = xm * y[:, :, None, None]
        out = jnp.einsum('nchw,oc->nohw', x_se, w1x1[:, :, 0, 0]) + b1x1[None, :, None, None]
        return out + x

    def _gn(v, G=32, eps=1e-5):
        B_, C_, H_, W_ = v.shape
        g = v.reshape(B_, G, C_ // G, H_, W_)
        m = jnp.mean(g, axis=(2, 3, 4), keepdims=True)
        s = jnp.var(g, axis=(2, 3, 4), keepdims=True)
        return ((g - m) / jnp.sqrt(s + eps)).reshape(v.shape)

    def _ln_c(v, eps=1e-6):
        m = jnp.mean(v, axis=1, keepdims=True)
        s = jnp.var(v, axis=1, keepdims=True)
        return (v - m) / jnp.sqrt(s + eps)

    def _ln_t(v, eps=1e-5):
        m = jnp.mean(v, axis=-1, keepdims=True)
        s = jnp.var(v, axis=-1, keepdims=True)
        return (v - m) / jnp.sqrt(s + eps)

    def _to_tokens(v):
        B_, C_, H_, W_ = v.shape
        return v.reshape(B_, C_, H_ * W_).transpose(0, 2, 1)
    def _from_tokens(t, like):
        B_, C_, H_, W_ = like.shape
        return t.transpose(0, 2, 1).reshape(B_, C_, H_, W_)

    x = _L0_conv_ref(x, L0_conv_w7, L0_conv_b7, L0_conv_w5, L0_conv_b5, L0_conv_w3, L0_conv_b3, L0_conv_fc1_w, L0_conv_fc1_b, L0_conv_fc2_w, L0_conv_fc2_b, L0_conv_w1x1, L0_conv_b1x1)
    return x


_drawn_inputs = setup_inputs


def setup_inputs(seed=0):
    import zlib

    import numpy as np

    out = dict(_drawn_inputs(seed))
    spreads = {'L0_conv_b1x1': (0.0, 0.1)}
    factors = {'L0_conv_b7': 5.465,
     'L0_conv_b5': 6.034,
     'L0_conv_b3': 5.224,
     'L0_conv_fc1_b': 64.0,
     'L0_conv_fc2_b': 8.0,
     'L0_conv_fc1_w': 8.0,
     'L0_conv_fc2_w': 8.0}
    for name, (base, spread) in spreads.items():
        noise = np.random.default_rng([zlib.crc32(name.encode()), seed]).standard_normal(out[name].shape)
        drawn = base * np.exp(spread * noise) if base else spread * noise
        out[name] = jnp.asarray(drawn.astype(out[name].dtype))
    for name, factor in factors.items():
        out[name] = (out[name] * factor).astype(out[name].dtype)
    return out
```

```python
import concourse.bass as bass
from concourse import mybir
from contextlib import ExitStack


def conv_se_kernel(nc, x, w7, b7, w5, b5, w3, b3, fc1_w, fc1_b, fc2_w, fc2_b, w1x1, b1x1, out):
    f32 = mybir.dt.float32
    f32r = mybir.dt.float32r
    ALU = mybir.AluOpType
    ACT = mybir.ActivationFunctionType
    ds = bass.ds

    N, C, H, W = x.shape
    R = fc1_w.shape[0]
    KS = w7.shape[-1]
    PAD = KS // 2
    B32 = 32
    WO = B32 - (KS - 1)
    J = -(-W // WO)
    JT = W - (J - 1) * WO
    XW = (J - 1) * WO + B32
    GQ = 4
    KH = 2
    KK = H // GQ // KH
    K = KH * KK
    NI = 4
    GROUPS = N // NI
    DK = 3
    WC = DK * GQ * WO
    HW2 = H * W // KH
    BLK = 16
    KKC = KK // BLK
    TILE = KKC * W
    CH = GQ * TILE
    P = 128
    STEPS = GROUPS * C
    BLOCKS = STEPS // BLK
    LAG = C // BLK

    zscr = nc.dram_tensor("z_scratch", (C, KH, N, GQ, KK, W), f32).ap()
    wscr = nc.dram_tensor("band_scratch", (C, P, WC), f32).ap()

    x_rows = x.rearrange("n c (h k g) w -> c h g k n w", h=KH, k=KK, g=GQ)
    z_rows = zscr.rearrange("c h n g k w -> c h (g k) n w")
    z_chan = zscr.rearrange("c h n g k w -> n (c h) g (k w)")
    x_chan = x.rearrange("n c (h r) w -> n (c h) (r w)", h=KH)
    out_chan = out.rearrange("n c (h r) w -> n (c h) (r w)", h=KH)

    ctx = ExitStack()
    with ctx:
        def sb(name, shape, dt=f32):
            return ctx.enter_context(nc.sbuf_tensor(name, shape, dt))

        def pb(name, shape):
            return ctx.enter_context(nc.psum_tensor(name, shape, f32))

        def sem(name):
            return ctx.enter_context(nc.semaphore(name))

        xin = sb("xin", [P, 2, NI, KH, XW])
        xT = sb("xT", [P, 2, 2, J, K])
        hi = sb("hi", [P, 2, 2, 2, J, K + 2], f32r)
        lo = sb("lo", [P, 2, 2, 2, J, K + 2], f32r)
        wraw = sb("wraw", [P, 2, WC])
        whi = sb("whi", [P, 2, DK, GQ, B32], f32r)
        wlo = sb("wlo", [P, 2, DK, GQ, B32], f32r)
        zt = sb("zt", [P, 2, KH, J, B32])
        zrow = sb("zrow", [P, 2, NI, KH, W])
        sum_a = sb("sum_a", [P, STEPS, NI])
        sum_b = sb("sum_b", [P, STEPS, NI])
        mixbuf = sb("mixbuf", [P, 3, 2, CH])
        zin, xres, oout = mixbuf[:, 0], mixbuf[:, 1], mixbuf[:, 2]
        zhi = sb("zhi", [P, 2, CH], f32r)
        zlo = sb("zlo", [P, 2, CH], f32r)
        band = bass.AP(mixbuf, 0, [[3 * 2 * CH, P], [GQ * WO, C], [1, GQ * WO]])
        w2 = sb("w2", [P, P])
        w2hi = sb("w2hi", [P, P], f32r)
        w2lo = sb("w2lo", [P, P], f32r)
        obias = sb("obias", [P, 1])
        cur = sb("cur", [P, C])
        mean = sb("mean", [C, 1])
        hid = sb("hid", [R, 1])
        gate = sb("gate", [P, 1])
        ident = sb("ident", [C, C])
        dup = sb("dup", [C, C, KH])
        taps = sb("taps", [KS * KS, 16, B32])
        even = sb("even", [P, C])
        half0 = sb("half0", [P, 1])
        half1 = sb("half1", [P, 1])
        ones = sb("ones", [P, 1])
        k7 = sb("k7", [C, KS, KS])
        k5 = sb("k5", [C, 5, 5])
        k3 = sb("k3", [C, 3, 3])
        bdw = sb("bdw", [C, 3])
        vecs = sb("vecs", [C, 3])
        vecd = sb("vecd", [P, 3])
        kT = sb("kT", [KS * KS, C])
        fc1s = sb("fc1s", [R, C])
        fc1b = sb("fc1b", [R, 1])
        fc1T = sb("fc1T", [C, P])
        fc2s = sb("fc2s", [C, R])
        fc2T = sb("fc2T", [R, P])
        w1s = sb("w1s", [C, C])
        w1d = sb("w1d", [C, C, KH])
        wbase = sb("wbase", [P, C, KH])

        ps_conv = pb("ps_conv", [P, 2, KH, 512])
        ps_mix = pb("ps_mix", [P, 2, 512])
        ps_se = pb("ps_se", [P, 512])

        params_loaded = sem("params_loaded")
        consts_made = sem("consts_made")
        pads_zeroed = sem("pads_zeroed")
        kern_summed = sem("kern_summed")
        bias_summed = sem("bias_summed")
        small_mm = sem("small_mm")
        small_copied = sem("small_copied")
        band_mm = sem("band_mm")
        band_copied_act = sem("band_copied_act")
        band_copied_dve = sem("band_copied_dve")
        band_stored = sem("band_stored")

        x_loaded = [sem("x_loaded0"), sem("x_loaded1")]
        w_loaded = [sem("w_loaded0"), sem("w_loaded1")]
        xT_done = sem("xT_done")
        hi_done = sem("hi_done")
        lo_done = sem("lo_done")
        whi_done = sem("whi_done")
        wlo_done = sem("wlo_done")
        conv_done = sem("conv_done")
        zt_done = sem("zt_done")
        zrow_done = sem("zrow_done")
        z_stored = [sem("z_stored0"), sem("z_stored1")]

        z_loaded = [sem("z_loaded0"), sem("z_loaded1")]
        res_loaded = [sem("res_loaded0"), sem("res_loaded1")]
        zhi_done = sem("zhi_done")
        zlo_done = sem("zlo_done")
        mix_done = sem("mix_done")
        out_done = sem("out_done")
        out_stored = [sem("out_stored0"), sem("out_stored1")]

        cur_done = sem("cur_done")
        se_sum = sem("se_sum")
        mean_done = sem("mean_done")
        se_fc1 = sem("se_fc1")
        hid_done = sem("hid_done")
        se_fc2 = sem("se_fc2")
        gate_done = sem("gate_done")
        w2_done = sem("w2_done")
        w2hi_done = sem("w2hi_done")
        w2lo_done = sem("w2lo_done")
        se_bias = sem("se_bias")
        obias_done = sem("obias_done")

        def need(eng, s, v):
            if not isinstance(v, int) or v > 0:
                eng.wait_ge(s, v)

        def run(engine, step):
            def block(b, conv, first=False, last=False):
                step(b * BLK, 0, b - LAG, conv, True, 0, 2)
                if first:
                    step(b * BLK + 1, 1, b - LAG, conv, True, 1, 2)
                    step(b * BLK + 2, 2, b - LAG, conv, True, 2, 2)
                with engine.Fori(1 if first else 0, BLK // 2 - (2 if last else 1)) as pair:
                    for s in (1, 2):
                        q = 2 * pair + s
                        step(b * BLK + q, q, b - LAG, conv, True, s, 2)
                if last:
                    step(b * BLK + BLK - 3, BLK - 3, b - LAG, conv, True, 1, 2)
                    step(b * BLK + BLK - 2, BLK - 2, b - LAG, conv, True, 2, 1)
                step(b * BLK + BLK - 1, BLK - 1, b - LAG, conv, True, BLK - 1, 0 if last else 2)

            step(0, 0, 0, True, False, 0, 2)
            step(1, 1, 0, True, False, 1, 2)
            with engine.Fori(1, C // 2) as pair:
                step(2 * pair, 0, 0, True, False, 2, 2)
                step(2 * pair + 1, 0, 0, True, False, 1, 2)
            block(LAG, True, first=True)
            with engine.Fori(LAG + 1, BLOCKS - 1) as b:
                block(b, True)
            block(BLOCKS - 1, True, last=True)
            with engine.Fori(BLOCKS, BLOCKS + LAG) as b:
                block(b, False)

        NBANK = GQ * WO // 8
        block_ = ctx.enter_context(nc.Block())

        @block_.sync
        def _(sp):
            col = lambda v: v.rearrange("(c a) -> c a", a=1)
            for dst, src in ((k7[:, :, :], w7[:, 0]), (k5[:, :, :], w5[:, 0]), (k3[:, :, :], w3[:, 0]),
                             (bdw[:, 0:1], col(b7)), (bdw[:, 1:2], col(b5)), (bdw[:, 2:3], col(b3)),
                             (vecs[:, 1:2], col(b1x1)), (vecs[:, 2:3], col(fc2_b)),
                             (fc1s[:, :], fc1_w), (fc1b[:, :], col(fc1_b)), (fc2s[:, :], fc2_w),
                             (w1s[:, :], w1x1[:, :, 0, 0])):
                sp.dma_start(dst, src).then_inc(params_loaded, 16)

            def load_x(t, par):
                n0, c = t // C * NI, t % C
                for h in range(KH):
                    for g in (0, 2, 1, 3):
                        sp.dma_start(xin[B32 * g:B32 * g + B32, par, :, h, PAD:PAD + W],
                                     x_rows[c, h, g, :, ds(n0, NI), :]).then_inc(x_loaded[par], 16)

            def load_w(t, par):
                sp.dma_start(wraw[:, par, :], wscr[t % C, :, :]).then_inc(w_loaded[par], 16)

            load_x(0, 0)
            load_x(1, 1)
            for dk in range(DK):
                sp.wait_ge(band_copied_act, dk * 6 + 6)
                sp.wait_ge(band_copied_dve, dk * 7 + 7)
                sp.dma_start(wscr[:, :, dk * GQ * WO:(dk + 1) * GQ * WO].rearrange("c p m -> p c m"),
                             band).then_inc(band_stored, 16)
            sp.wait_ge(band_stored, DK * 16)
            load_w(0, 0)
            load_w(1, 1)

            def load_z(n, tau, s, par):
                need(sp, zhi_done, 2 * tau - 2)
                need(sp, zlo_done, 2 * tau - 2)
                sp.dma_start(zin[:, par].rearrange("p (g a) -> p g a", g=GQ),
                             z_chan[n, :, :, ds(s * TILE, TILE)]).then_inc(z_loaded[par], 16)

            def load_res(n, tau, s, par):
                need(sp, out_done, 4 * tau - 4)
                sp.dma_start(xres[:, par], x_chan[n, :, ds(s * CH, CH)]).then_inc(res_loaded[par], 16)

            def step(t, q, n, conv, mix, s, left):
                par = s % 2
                if conv and left == 2:
                    sp.wait_ge(xT_done, 4 * t + 4)
                    load_x(t + 2, par)
                    sp.wait_ge(whi_done, t + 1)
                    sp.wait_ge(wlo_done, t + 1)
                    load_w(t + 2, par)
                if mix:
                    tau = t - C
                    if s == 0:
                        sp.wait_ge(z_stored[0], 16 * KH * (t // 2 if conv else STEPS // 2))
                        sp.wait_ge(z_stored[1], 16 * KH * (t // 2 if conv else STEPS // 2))
                        load_z(n, tau, 0, 0)
                        load_res(n, tau, 0, 0)
                    if s < BLK - 1:
                        load_z(n, tau + 1, q + 1, 1 - par)
                        load_res(n, tau + 1, q + 1, 1 - par)
                if conv:
                    sp.wait_ge(zrow_done, 8 * t + 8)
                    for h in range(KH):
                        sp.dma_start(z_rows[t % C, h, :, ds(t // C * NI, NI), :],
                                     zrow[:, par, :, h, :]).then_inc(z_stored[par], 16)
                if mix:
                    sp.wait_ge(out_done, 4 * tau + 4)
                    sp.dma_start(out_chan[n, :, ds(q * CH, CH)], oout[:, par]).then_inc(out_stored[par], 16)

            run(sp, step)
            sp.wait_ge(out_stored[0], 16 * N * BLK // 2)
            sp.wait_ge(out_stored[1], 16 * N * BLK // 2)

        @block_.gpsimd
        def _(pool):
            def zero(ap):
                nc.gpsimd.memset(ap, 0.0).then_inc(consts_made, 1)

            zero(ident[:, :])
            zero(dup[:, :, :])
            zero(taps[:, :, :])
            zero(even[:, :])
            zero(fc1T[:, :])
            nc.gpsimd.memset(ones[:, :], 1.0).then_inc(consts_made, 1)
            pool.wait_ge(consts_made, 6)
            for ap, pattern, cm in ((ident[:, :], [[-1, C]], 1), (dup[:, :, :], [[-1, C], [0, KH]], 1),
                                    (taps[:, 5:5 + KS, 0:KS], [[-KS, KS], [-1, KS]], 1),
                                    (even[:, :], [[-2, C]], 1)):
                nc.gpsimd.affine_select(out=ap, in_=ap, compare_op=ALU.not_equal, fill=1.0, base=0,
                                        pattern=pattern, channel_multiplier=cm).then_inc(consts_made, 1)

            def lo_half(t, par, h):
                pool.wait_ge(hi_done, 2 * t + h + 1)
                nc.gpsimd.tensor_tensor(
                    lo[:, par, h, :, :, 1:K + 1].rearrange("p n j k -> p (n j) k"),
                    xT[:, h].rearrange("p n j k -> p (n j) k"),
                    hi[:, par, h, :, :, 1:K + 1].bitcast(f32).rearrange("p n j k -> p (n j) k"),
                    ALU.subtract).then_inc(lo_done, 1)

            def w_lo(t, par):
                pool.wait_ge(whi_done, t + 1)
                nc.gpsimd.tensor_tensor(
                    wlo[:, par, :, :, 0:WO].rearrange("p d g m -> p (d g) m"),
                    wraw[:, par].rearrange("p (a m) -> p a m", m=WO),
                    whi[:, par, :, :, 0:WO].bitcast(f32).rearrange("p d g m -> p (d g) m"),
                    ALU.subtract).then_inc(wlo_done, 1)

            def z_lo(tau, par):
                for h in range(2):
                    pool.wait_ge(zhi_done, 2 * tau + h + 1)
                    a, b = h * CH // 2, (h + 1) * CH // 2
                    nc.gpsimd.tensor_tensor(zlo[:, par, a:b], zin[:, par, a:b], zhi[:, par, a:b].bitcast(f32),
                                            ALU.subtract).then_inc(zlo_done, 1)

            def step(t, q, n, conv, mix, s, left):
                par = s % 2
                if mix and s:
                    z_lo(t - C, par)
                if conv and left:
                    lo_half(t + 1, 1 - par, 0)
                    w_lo(t + 1, 1 - par)
                    lo_half(t + 1, 1 - par, 1)
                if mix and not s:
                    z_lo(t - C, par)

            pool.wait_ge(pads_zeroed, 7)
            lo_half(0, 0, 0)
            w_lo(0, 0)
            lo_half(0, 0, 1)
            run(pool, step)

        @block_.scalar
        def _(act):
            act.wait_ge(consts_made, 10)
            nc.scalar.activation(gate[:, :], ones[:, :], ACT.Sigmoid).then_inc(gate_done, 1)

            def band_copy(q):
                dk, j = q // NBANK, q % NBANK
                act.wait_ge(band_mm, q + 1)
                if j == 1 and dk:
                    act.wait_ge(band_stored, 16 * dk)
                nc.scalar.activation(band[:, :, 8 * j:8 * j + 8],
                                     ps_conv[:, q % 4 // 2, q % 2, :].rearrange("p (i c) -> p c i", c=C),
                                     ACT.Copy).then_inc(band_copied_act, 1)

            for q in range(DK * NBANK):
                if q % NBANK % 2:
                    band_copy(q)

            def hi_half(t, par, h):
                act.wait_ge(xT_done, 4 * t + 2 * h + 2)
                need(act, conv_done, 4 * t + 2 * h - 6)
                nc.scalar.activation(hi[:, par, h, :, :, 1:K + 1].rearrange("p n j k -> p (n j) k"),
                                     xT[:, h].rearrange("p n j k -> p (n j) k"), ACT.Copy).then_inc(hi_done, 1)

            def w_hi(t, par):
                need(act, conv_done, 4 * t - 4)
                act.wait_ge(w_loaded[par], 16 * (t // 2) + 16)
                nc.scalar.activation(whi[:, par, :, :, 0:WO].rearrange("p d g m -> p (d g) m"),
                                     wraw[:, par].rearrange("p (a m) -> p a m", m=WO),
                                     ACT.Copy).then_inc(whi_done, 1)

            def pack(t, par, i):
                act.wait_ge(zt_done, 4 * t + i + 1)
                if i == 0:
                    need(act, z_stored[par], 16 * KH * (t // 2))
                JW = (J - 1) * WO
                nc.scalar.activation(
                    zrow[:, par, i, :, 0:JW].rearrange("p h (j m) -> p h j m", m=WO),
                    zt[:, i % 2, :, 0:J - 1, 0:WO], ACT.Copy,
                    accum_out=sum_a[:, ds(t, 1), i]).then_inc(zrow_done, 1)
                nc.scalar.activation(
                    zrow[:, par, i, :, JW:W], zt[:, i % 2, :, J - 1, 0:JT], ACT.Copy,
                    accum_out=sum_b[:, ds(t, 1), i]).then_inc(zrow_done, 1)

            def z_hi(tau, par):
                act.wait_ge(z_loaded[par], 16 * (tau // 2) + 16)
                need(act, mix_done, 4 * tau - 4)
                for h in range(2):
                    a, b = h * CH // 2, (h + 1) * CH // 2
                    nc.scalar.activation(zhi[:, par, a:b], zin[:, par, a:b], ACT.Copy).then_inc(zhi_done, 1)

            def step(t, q, n, conv, mix, s, left):
                par = s % 2
                if mix and s:
                    z_hi(t - C, par)
                if conv:
                    pack(t, par, 0)
                    if left:
                        hi_half(t + 1, 1 - par, 0)
                        w_hi(t + 1, 1 - par)
                    pack(t, par, 1)
                    if left:
                        hi_half(t + 1, 1 - par, 1)
                    pack(t, par, 2)
                if mix and not s:
                    act.wait_ge(se_fc2, n + 1)
                    nc.scalar.activation(gate[:, :], ps_se[:, 2:3], ACT.Sigmoid,
                                         bias=vecd[:, 2:3]).then_inc(gate_done, 1)
                    act.wait_ge(w2_done, n + 1)
                    need(act, mix_done, 4 * (t - C))
                    nc.scalar.activation(w2hi[:, :], w2[:, :], ACT.Copy).then_inc(w2hi_done, 1)
                if conv:
                    pack(t, par, 3)
                if mix and not s:
                    z_hi(t - C, par)

            act.wait_ge(pads_zeroed, 7)
            hi_half(0, 0, 0)
            w_hi(0, 0)
            hi_half(0, 0, 1)
            run(act, step)

        @block_.vector
        def _(dve):
            for ap in (xin[:, :, :, :, 0:PAD].rearrange("p b n h w -> p (b n h) w"),
                       xin[:, :, :, :, PAD + W:XW].rearrange("p b n h w -> p (b n h) w"),
                       *(b[:, :, :, :, :, 0:K + 2:K + 1].bitcast(f32).rearrange("p a b n j k -> p (a b n j) k")
                         for b in (hi, lo)),
                       whi[:, :, :, :, WO:B32].bitcast(f32).rearrange("p a d g m -> p (a d g) m"),
                       wlo[:, :, :, :, WO:B32].bitcast(f32).rearrange("p a d g m -> p (a d g) m"),
                       w2[:, :]):
                nc.vector.memset(ap, 0.0).then_inc(pads_zeroed, 1)

            dve.wait_ge(params_loaded, 12 * 16)
            dve.wait_ge(pads_zeroed, 7)
            nc.vector.tensor_tensor(k7[:, 1:6, 1:6], k7[:, 1:6, 1:6], k5[:, :, :], ALU.add).then_inc(kern_summed, 1)
            dve.wait_ge(kern_summed, 1)
            nc.vector.tensor_tensor(k7[:, 2:5, 2:5], k7[:, 2:5, 2:5], k3[:, :, :], ALU.add).then_inc(kern_summed, 1)
            nc.vector.tensor_tensor(vecs[:, 0:1], bdw[:, 0:1], bdw[:, 1:2], ALU.add).then_inc(bias_summed, 1)
            dve.wait_ge(bias_summed, 1)
            nc.vector.tensor_tensor(vecs[:, 0:1], vecs[:, 0:1], bdw[:, 2:3], ALU.add).then_inc(bias_summed, 1)
            dve.wait_ge(consts_made, 10)
            for h in range(KH):
                nc.vector.tensor_copy(w1d[:, :, h], w1s[:, :]).then_inc(bias_summed, 1)
            nc.vector.reduce_sum(half0[:, :], even[:, :], axis=mybir.AxisListType.X).then_inc(bias_summed, 1)
            dve.wait_ge(bias_summed, 5)
            nc.vector.tensor_scalar(half1[:, :], half0[:, :], -1.0, 1.0, ALU.mult, ALU.add).then_inc(bias_summed, 1)
            dve.wait_ge(bias_summed, 6)
            dve.wait_ge(small_mm, 5)
            nc.vector.tensor_copy(kT[:, :], ps_se[0:KS * KS, 0:C]).then_inc(small_copied, 1)
            nc.vector.tensor_copy(fc1T[:, 0:R], ps_se[0:C, 64:64 + R]).then_inc(small_copied, 1)
            nc.vector.tensor_copy(fc2T[:, :], ps_se[0:R, 128:256]).then_inc(small_copied, 1)
            nc.vector.tensor_copy(vecd[:, :], ps_se[:, 256:259]).then_inc(small_copied, 1)
            for h, halfh in enumerate((half0, half1)):
                nc.vector.tensor_scalar(wbase[:, :, h],
                                        ps_mix[:, 0, 0:P].rearrange("p (c h) -> p c h", h=KH)[:, :, h],
                                        halfh[:, 0:1], None, ALU.mult).then_inc(small_copied, 1)

            def band_copy(q):
                dk, j = q // NBANK, q % NBANK
                dve.wait_ge(band_mm, q + 1)
                if j == 0 and dk:
                    dve.wait_ge(band_stored, 16 * dk)
                nc.vector.tensor_copy(band[:, :, 8 * j:8 * j + 8],
                                      ps_conv[:, q % 4 // 2, q % 2, :].rearrange("p (i c) -> p c i", c=C)
                                      ).then_inc(band_copied_dve, 1)

            for q in range(DK * NBANK):
                if q % NBANK % 2 == 0:
                    band_copy(q)

            def patches(t, par, h):
                if h == 0:
                    dve.wait_ge(x_loaded[par], 128 * (t // 2) + 128)
                need(dve, hi_done, 2 * t + h - 1)
                need(dve, lo_done, 2 * t + h - 1)
                for kh in range(KH):
                    src = bass.AP(xin, (par * NI + 2 * h) * KH * XW + kh * XW,
                                  [[2 * NI * KH * XW, P], [KH * XW, 2], [WO, J], [1, B32]])
                    nc.vector.transpose(xT[:, h, :, :, kh * KK:kh * KK + KK], src).then_inc(xT_done, 1)

            def rows(t, i):
                dve.wait_ge(conv_done, 4 * t + i + 1)
                need(dve, zrow_done, 2 * (4 * t + i - 1))
                nc.vector.transpose(zt[:, i % 2].rearrange("p h j m -> p h (j m)"),
                                    ps_conv[:, i % 2, :, 0:J * KK]).then_inc(zt_done, 1)

            def add(tau, par, i):
                if i == 0:
                    dve.wait_ge(res_loaded[par], 16 * (tau // 2) + 16)
                    need(dve, out_stored[par], 16 * (tau // 2))
                dve.wait_ge(mix_done, 4 * tau + i + 1)
                pick = lambda buf: buf[:, par].rearrange("p (k g w) -> p g k w", g=GQ, w=W)[:, i]
                nc.vector.scalar_tensor_tensor(
                    out=pick(oout), in0=ps_mix[:, i % 2, :].rearrange("p (k w) -> p k w", w=W),
                    scalar=obias[:, 0:1], in1=pick(xres), op0=ALU.add, op1=ALU.add).then_inc(out_done, 1)

            def step(t, q, n, conv, mix, s, left):
                par = s % 2
                head = mix and s == 0
                tau = t - C
                if head:
                    dve.wait_ge(zrow_done, 8 * (t if conv else STEPS))
                    need(dve, se_sum, n)
                    grp, im = n // NI, n % NI
                    pick = lambda s_: s_[:, ds(grp * C, C), ds(im, 1)].rearrange("p c a -> p (c a)")
                    nc.vector.tensor_tensor(cur[:, :], pick(sum_a), pick(sum_b), ALU.add).then_inc(cur_done, 1)
                if conv:
                    if left:
                        patches(t + 1, 1 - par, 0)
                    rows(t, 0)
                if head:
                    dve.wait_ge(se_sum, n + 1)
                    nc.vector.tensor_scalar(mean[:, :], ps_se[0:C, 0:1], 1.0 / (H * W), vecs[:, 0:1],
                                            ALU.mult, ALU.add).then_inc(mean_done, 1)
                if conv:
                    rows(t, 1)
                    if mix and not head:
                        add(tau, par, 0)
                if head:
                    dve.wait_ge(se_fc1, n + 1)
                    nc.vector.tensor_scalar(hid[:, :], ps_se[0:R, 1:2], fc1b[:, 0:1], 0.0,
                                            ALU.add, ALU.max).then_inc(hid_done, 1)
                if conv:
                    if left:
                        patches(t + 1, 1 - par, 1)
                    rows(t, 2)
                    if mix and not head:
                        add(tau, par, 1)
                if head:
                    dve.wait_ge(gate_done, n + 2)
                    need(dve, se_bias, n)
                    nc.vector.tensor_scalar(w2[:, :], wbase[:, :, :].rearrange("p c h -> p (c h)"), gate[:, 0:1],
                                            None, ALU.mult).then_inc(w2_done, 1)
                    dve.wait_ge(w2_done, n + 1)
                    dve.wait_ge(w2hi_done, n + 1)
                    nc.vector.tensor_tensor(w2lo[:, :], w2[:, :], w2hi[:, :].bitcast(f32),
                                            ALU.subtract).then_inc(w2lo_done, 1)
                if conv:
                    rows(t, 3)
                if head:
                    dve.wait_ge(se_bias, n + 1)
                    nc.vector.tensor_scalar(obias[:, :], ps_se[:, 3:4], vecd[:, 1:2], None,
                                            ALU.add).then_inc(obias_done, 1)
                    dve.wait_ge(obias_done, n + 1)
                if mix:
                    for i in range(2 if conv and not head else 0, 4):
                        add(tau, par, i)

            patches(0, 0, 0)
            patches(0, 0, 1)
            run(dve, step)

        @block_.tensor
        def _(pe):
            mm = nc.tensor.matmul
            pe.wait_ge(kern_summed, 2)
            pe.wait_ge(bias_summed, 6)
            dupm = dup[:, :, :].rearrange("p c h -> p (c h)")
            for o, a, b in ((ps_se[0:KS * KS, 0:C], k7[:, :, :].rearrange("p a b -> p (a b)"), ident[:, :]),
                            (ps_se[0:C, 64:64 + R], fc1s[:, :], ident[0:R, 0:R]),
                            (ps_se[0:R, 128:256], fc2s[:, :], dupm),
                            (ps_se[:, 256:259], dupm, vecs[:, :]),
                            (ps_mix[:, 0, 0:P], w1d[:, :, :].rearrange("p c h -> p (c h)"), dupm)):
                mm(o, a, b, start=True, stop=True).then_inc(small_mm, 1)

            pe.wait_ge(small_copied, 6)
            q = 0
            for dk in range(DK):
                for j in range(NBANK):
                    if q >= 4:
                        r = q - 4
                        if r % NBANK % 2:
                            pe.wait_ge(band_copied_act, r // NBANK * 6 + (r % NBANK + 1) // 2)
                        else:
                            pe.wait_ge(band_copied_dve, r // NBANK * 7 + r % NBANK // 2 + 1)
                    for i in range(8):
                        gout, m = (8 * j + i) // WO, (8 * j + i) % WO
                        at = (4 * (dk - 1) - gout + 8) * B32 - m
                        last = mm(ps_conv[:, q % 4 // 2, q % 2, i * C:(i + 1) * C],
                                  taps[:, :, :].rearrange("k a q -> k (a q)")[:, at:at + P], kT[:, :], start=True, stop=True)
                    last.then_inc(band_mm, 1)
                    q += 1

            def conv_image(t, par, i):
                h, n = i // 2, i % 2
                if i == 0:
                    pe.wait_ge(wlo_done, t + 1)
                if n == 0:
                    pe.wait_ge(lo_done, 2 * t + h + 1)
                need(pe, zt_done, 4 * t + i - 1)
                terms = [(w, src, dk) for dk in (1, 0, 2) for w, src in ((whi, hi), (whi, lo), (wlo, hi))]
                for m, (w, src, dk) in enumerate(terms):
                    for kh in range(KH):
                        last = mm(ps_conv[:, i % 2, kh, 0:J * KK], w[:, par, dk].rearrange("p g m -> p (g m)"),
                                  src[:, par, h, n, :, kh * KK + dk:kh * KK + dk + KK],
                                  start=(m == 0), stop=(m == len(terms) - 1))
                last.then_inc(conv_done, 1)

            def mix_tile(tau, par, i):
                if i % 2 == 0:
                    pe.wait_ge(zlo_done, 2 * tau + i // 2 + 1)
                need(pe, out_done, 4 * tau + i - 1)
                a = i * TILE
                for m, (w, src) in enumerate(((w2hi, zhi), (w2hi, zlo), (w2lo, zhi))):
                    last = mm(ps_mix[:, i % 2, :], w[:, :], src[:, par, a:a + TILE], start=(m == 0), stop=(m == 2))
                last.then_inc(mix_done, 1)

            def step(t, q, n, conv, mix, s, left):
                par = s % 2
                tau = t - C
                if not (mix and s == 0):
                    order = ("c0", "c1", "m0", "c2", "m1", "c3", "m2", "m3")
                    for what in order:
                        i = int(what[1])
                        if what[0] == "c" and conv:
                            conv_image(t, par, i)
                        if what[0] == "m" and mix:
                            mix_tile(tau, par, i)
                    return
                if conv:
                    conv_image(t, par, 0)
                pe.wait_ge(cur_done, n + 1)
                mm(ps_se[0:C, 0:1], cur[:, :], ones[:, :], start=True, stop=True).then_inc(se_sum, 1)
                if conv:
                    conv_image(t, par, 1)
                pe.wait_ge(mean_done, n + 1)
                mm(ps_se[:, 1:2], fc1T[:, :], mean[:, :], start=True, stop=True).then_inc(se_fc1, 1)
                if conv:
                    conv_image(t, par, 2)
                pe.wait_ge(hid_done, n + 1)
                mm(ps_se[:, 2:3], fc2T[:, :], hid[:, :], start=True, stop=True).then_inc(se_fc2, 1)
                if conv:
                    conv_image(t, par, 3)
                pe.wait_ge(w2_done, n + 1)
                mm(ps_se[:, 3:4], w2[:, :], vecd[:, 0:1], start=True, stop=True).then_inc(se_bias, 1)
                pe.wait_ge(w2lo_done, n + 1)
                for i in range(4):
                    mix_tile(tau, par, i)

            run(pe, step)


_INS = ["x", "L0_conv_w7", "L0_conv_b7", "L0_conv_w5", "L0_conv_b5", "L0_conv_w3", "L0_conv_b3", "L0_conv_fc1_w",
        "L0_conv_fc1_b", "L0_conv_fc2_w", "L0_conv_fc2_b", "L0_conv_w1x1", "L0_conv_b1x1"]


def kernel(**inputs):
    import numpy as _np
    import concourse.bacc as _bacc
    from concourse import mybir as _mybir
    from concourse.bass_utils import run_bass_kernel_spmd as _run

    nc = _bacc.Bacc("TRN2", target_bir_lowering=False, num_devices=1)
    arrays, args = {}, []
    for name in _INS:
        a = _np.ascontiguousarray(inputs[name])
        arrays[f"in_{name}_dram"] = a
        args.append(nc.dram_tensor(f"in_{name}_dram", a.shape, _mybir.dt.from_np(a.dtype), kind="ExternalInput").ap())
    shape = inputs["x"].shape
    args.append(nc.dram_tensor("out_0_dram", shape, _mybir.dt.float32, kind="ExternalOutput").ap())
    conv_se_kernel(nc, *args)
    r = _run(nc, [arrays], core_ids=[0])
    return r.results[0]["out_0_dram"]
```

```python
import concourse.bass as bass
from concourse import mybir
from contextlib import ExitStack


def conv_se_kernel(nc, x, w7, b7, w5, b5, w3, b3, fc1_w, fc1_b, fc2_w, fc2_b, w1x1, b1x1, out):
    f32 = mybir.dt.float32
    f32r = mybir.dt.float32r
    ALU = mybir.AluOpType
    ACT = mybir.ActivationFunctionType
    ds = bass.ds

    N, C, H, W = x.shape
    R = fc1_w.shape[0]
    KS = w7.shape[-1]
    PAD = KS // 2
    B32 = 32
    WO = B32 - (KS - 1)
    J = -(-W // WO)
    JT = W - (J - 1) * WO
    XW = (J - 1) * WO + B32
    GQ = 4
    KH = 2
    KK = H // GQ // KH
    K = KH * KK
    NC = 4
    DK = 3
    BANDS = DK * GQ
    HW2 = H * W // KH
    BLK = C // NC
    KKC = KK // BLK
    TILE = KKC * W
    CH = GQ * TILE
    P = 128
    STEPS = N * BLK

    zscr = nc.dram_tensor("z_scratch", (N, C, KH, GQ, KK, W), f32).ap()
    bscr = nc.dram_tensor("band_scratch", (C, B32, KS, WO), f32).ap()

    x_rows = x.rearrange("n c (h k g) w -> n g k (c h) w", h=KH, k=KK, g=GQ)
    z_rows = zscr.rearrange("n c h g k w -> n (g k) (c h) w")
    z_chan = zscr.rearrange("n c h g k w -> n (c h) g (k w)")
    b_chan = bscr.rearrange("c p a m -> p c (a m)")
    x_chan = x.rearrange("n c (h r) w -> n (c h) (r w)", h=KH)
    out_chan = out.rearrange("n c (h r) w -> n (c h) (r w)", h=KH)

    ctx = ExitStack()
    with ctx:
        def sb(name, shape, dt=f32):
            return ctx.enter_context(nc.sbuf_tensor(name, shape, dt))

        def pb(name, shape):
            return ctx.enter_context(nc.psum_tensor(name, shape, f32))

        def sem(name):
            return ctx.enter_context(nc.semaphore(name))

        xin = sb("xin", [P, 2, NC, KH, XW])
        xT = sb("xT", [P, 2, 2, J, K])
        hi = sb("hi", [P, 2, 2, 2, J, K + 2], f32r)
        lo = sb("lo", [P, 2, 2, 2, J, K + 2], f32r)
        wraw = sb("wraw", [B32, 2, NC, KS, WO])
        whi = sb("whi", [P, 2, NC, BANDS, B32], f32r)
        wlo = sb("wlo", [P, 2, NC, BANDS, B32], f32r)
        zt = sb("zt", [P, 2, KH, J, B32])
        zrow = sb("zrow", [P, 2, NC, KH, W])
        sum_a = sb("sum_a", [P, 2 * C])
        sum_b = sb("sum_b", [P, 2 * C])
        mixbuf = sb("mixbuf", [P, 3, 2, CH])
        zin, xres, oout = mixbuf[:, 0], mixbuf[:, 1], mixbuf[:, 2]
        zhi = sb("zhi", [P, CH], f32r)
        zlo = sb("zlo", [P, CH], f32r)
        bands = bass.AP(mixbuf, 0, [[3 * 2 * CH, C], [1, B32 * KS * WO]])
        band_taps = bass.AP(mixbuf, 0, [[3 * 2 * CH, C], [KS * WO + 1, WO], [KS * WO, KS], [WO, KS]])
        w2 = sb("w2", [P, P])
        w2hi = sb("w2hi", [P, P], f32r)
        w2lo = sb("w2lo", [P, P], f32r)
        obias = sb("obias", [P, 1])
        cur = sb("cur", [P, C])
        mean = sb("mean", [C, 1])
        hid = sb("hid", [R, 1])
        gate = sb("gate", [P, 1])
        ident = sb("ident", [C, C])
        dup = sb("dup", [C, C, KH])
        even = sb("even", [P, C])
        half0 = sb("half0", [P, 1])
        half1 = sb("half1", [P, 1])
        ones = sb("ones", [P, 1])
        k7 = sb("k7", [C, KS, KS])
        k5 = sb("k5", [C, 5, 5])
        k3 = sb("k3", [C, 3, 3])
        bdw = sb("bdw", [C, 3])
        vecs = sb("vecs", [C, 3])
        vecd = sb("vecd", [P, 3])
        fc1s = sb("fc1s", [R, C])
        fc1b = sb("fc1b", [R, 1])
        fc1T = sb("fc1T", [C, P])
        fc2s = sb("fc2s", [C, R])
        fc2T = sb("fc2T", [R, P])
        w1s = sb("w1s", [C, C])
        w1d = sb("w1d", [C, C, KH])
        wbase = sb("wbase", [P, C, KH])

        ps_conv = pb("ps_conv", [P, 2, KH, 512])
        ps_mix = pb("ps_mix", [P, 2, 512])
        ps_se = pb("ps_se", [P, 512])

        kern_loaded = sem("kern_loaded")
        params_loaded = sem("params_loaded")
        consts_made = sem("consts_made")
        pads_zeroed = sem("pads_zeroed")
        kern_summed = sem("kern_summed")
        bias_summed = sem("bias_summed")
        small_mm = sem("small_mm")
        small_copied = sem("small_copied")
        band_zeroed = sem("band_zeroed")
        band_made = sem("band_made")
        band_stored = sem("band_stored")

        x_loaded = [sem("x_loaded0"), sem("x_loaded1")]
        w_loaded = [sem("w_loaded0"), sem("w_loaded1")]
        xT_done = sem("xT_done")
        hi_done = sem("hi_done")
        lo_done = sem("lo_done")
        whi_done = sem("whi_done")
        wlo_done = sem("wlo_done")
        wlo_copied = sem("wlo_copied")
        conv_done = sem("conv_done")
        zt_done = sem("zt_done")
        zrow_done = sem("zrow_done")
        z_stored = [sem("z_stored0"), sem("z_stored1")]

        z_loaded = [sem("z_loaded0"), sem("z_loaded1")]
        res_loaded = [sem("res_loaded0"), sem("res_loaded1")]
        zhi_done = sem("zhi_done")
        zlo_done = sem("zlo_done")
        mix_done = sem("mix_done")
        out_done = sem("out_done")
        out_stored = [sem("out_stored0"), sem("out_stored1")]

        cur_done = sem("cur_done")
        se_sum = sem("se_sum")
        mean_done = sem("mean_done")
        se_fc1 = sem("se_fc1")
        hid_done = sem("hid_done")
        se_fc2 = sem("se_fc2")
        gate_done = sem("gate_done")
        w2_done = sem("w2_done")
        w2hi_done = sem("w2hi_done")
        w2lo_done = sem("w2lo_done")
        se_bias = sem("se_bias")
        obias_done = sem("obias_done")

        def need(eng, s, v):
            if not isinstance(v, int) or v > 0:
                eng.wait_ge(s, v)

        def run(engine, step):
            def block(b, conv, first=False, last=False):
                step(b * BLK, 0, b - 1, conv, True, 0, 2)
                if first:
                    step(b * BLK + 1, 1, b - 1, conv, True, 1, 2)
                    step(b * BLK + 2, 2, b - 1, conv, True, 2, 2)
                with engine.Fori(1 if first else 0, BLK // 2 - (2 if last else 1)) as pair:
                    for s in (1, 2):
                        q = 2 * pair + s
                        step(b * BLK + q, q, b - 1, conv, True, s, 2)
                if last:
                    step(b * BLK + BLK - 3, BLK - 3, b - 1, conv, True, 1, 2)
                    step(b * BLK + BLK - 2, BLK - 2, b - 1, conv, True, 2, 1)
                step(b * BLK + BLK - 1, BLK - 1, b - 1, conv, True, BLK - 1, 0 if last else 2)

            step(0, 0, -1, True, False, 0, 2)
            step(1, 1, -1, True, False, 1, 2)
            with engine.Fori(1, BLK // 2) as pair:
                step(2 * pair, 2 * pair, -1, True, False, 2, 2)
                step(2 * pair + 1, 2 * pair + 1, -1, True, False, 1, 2)
            block(1, True, first=True)
            with engine.Fori(2, N - 1) as b:
                block(b, True)
            block(N - 1, True, last=True)
            block(N, False)

        def blocks(w, g, par):
            return w[B32 * g:B32 * g + B32, par, :, GQ - g:GQ - g + KS, 0:WO]

        block_ = ctx.enter_context(nc.Block())

        @block_.sync
        def _(sp):
            col = lambda v: v.rearrange("(c a) -> c a", a=1)
            for dst, src in ((k7[:, :, :], w7[:, 0]), (k5[:, :, :], w5[:, 0]), (k3[:, :, :], w3[:, 0])):
                sp.dma_start(dst, src).then_inc(kern_loaded, 16)

            def load_x(n, q, par):
                for g in (0, 2, 1, 3):
                    sp.dma_start(xin[B32 * g:B32 * g + B32, par, :, :, PAD:PAD + W].rearrange("p c h w -> p (c h) w"),
                                 x_rows[n, g, :, ds(q * NC * KH, NC * KH), :]
                                 ).then_inc(x_loaded[par], 16)

            def load_w(q, par):
                sp.dma_start(wraw[:, par].rearrange("p c a m -> p c (a m)"),
                             b_chan[:, ds(q * NC, NC), :]).then_inc(w_loaded[par], 16)

            load_x(0, 0, 0)
            for dst, src in ((bdw[:, 0:1], col(b7)), (bdw[:, 1:2], col(b5)), (bdw[:, 2:3], col(b3)),
                             (vecs[:, 1:2], col(b1x1)), (vecs[:, 2:3], col(fc2_b)),
                             (fc1s[:, :], fc1_w), (fc1b[:, :], col(fc1_b)), (fc2s[:, :], fc2_w),
                             (w1s[:, :], w1x1[:, :, 0, 0])):
                sp.dma_start(dst, src).then_inc(params_loaded, 16)
            load_x(0, 1, 1)
            sp.wait_ge(band_made, 1)
            sp.dma_start(bscr.rearrange("c p a m -> c (p a m)"), bands).then_inc(band_stored, 16)
            sp.wait_ge(band_stored, 16)
            load_w(0, 0)
            load_w(1, 1)

            def load_z(n, tau, s, par):
                need(sp, zhi_done, 2 * tau - 2)
                need(sp, zlo_done, 2 * tau - 2)
                sp.dma_start(zin[:, par].rearrange("p (g a) -> p g a", g=GQ),
                             z_chan[n, :, :, ds(s * TILE, TILE)]).then_inc(z_loaded[par], 16)

            def load_res(n, tau, s, par):
                need(sp, out_done, 4 * tau - 4)
                sp.dma_start(xres[:, par], x_chan[n, :, ds(s * CH, CH)]).then_inc(res_loaded[par], 16)

            def step(t, q, n, conv, mix, s, left):
                par = s % 2
                if conv and left == 2:
                    n2, q2, done = (t + 2) // BLK, (t + 2) % BLK, t + 1
                    if not isinstance(t, int):
                        n2, q2, done = sp.snap(n2), sp.snap(q2), sp.snap(done)
                    sp.wait_ge(xT_done, 4 * t + 4)
                    load_x(n2, q2, par)
                    sp.wait_ge(wlo_done, done)
                    load_w(q2, par)
                if mix:
                    tau = t - BLK
                    if s == 0:
                        sp.wait_ge(z_stored[0], 16 * (t // 2))
                        sp.wait_ge(z_stored[1], 16 * (t // 2))
                        load_z(n, tau, 0, 0)
                        load_res(n, tau, 0, 0)
                    if s < BLK - 1:
                        load_z(n, tau + 1, q + 1, 1 - par)
                        load_res(n, tau + 1, q + 1, 1 - par)
                if conv:
                    sp.wait_ge(zrow_done, 8 * t + 8)
                    sp.dma_start(z_rows[n + 1, :, ds(q * NC * KH, NC * KH), :],
                                 zrow[:, par].rearrange("p c h w -> p (c h) w")).then_inc(z_stored[par], 16)
                if mix:
                    sp.wait_ge(out_done, 4 * tau + 4)
                    sp.dma_start(out_chan[n, :, ds(q * CH, CH)], oout[:, par]).then_inc(out_stored[par], 16)

            run(sp, step)
            sp.wait_ge(out_stored[0], 16 * N * BLK // 2)
            sp.wait_ge(out_stored[1], 16 * N * BLK // 2)

        @block_.gpsimd
        def _(pool):
            def zero(ap):
                nc.gpsimd.memset(ap, 0.0).then_inc(consts_made, 1)

            nc.gpsimd.memset(bands, 0.0).then_inc(band_zeroed, 1)
            zero(ident[:, :])
            zero(dup[:, :, :])
            zero(even[:, :])
            zero(fc1T[:, :])
            nc.gpsimd.memset(ones[:, :], 1.0).then_inc(consts_made, 1)
            pool.wait_ge(consts_made, 5)
            for ap, pattern, cm in ((ident[:, :], [[-1, C]], 1), (dup[:, :, :], [[-1, C], [0, KH]], 1),
                                    (even[:, :], [[-2, C]], 1)):
                nc.gpsimd.affine_select(out=ap, in_=ap, compare_op=ALU.not_equal, fill=1.0, base=0,
                                        pattern=pattern, channel_multiplier=cm).then_inc(consts_made, 1)

            def lo_half(t, par, h):
                pool.wait_ge(hi_done, 2 * t + h + 1)
                nc.gpsimd.tensor_tensor(
                    lo[:, par, h, :, :, 1:K + 1].rearrange("p n j k -> p (n j) k"),
                    xT[:, h].rearrange("p n j k -> p (n j) k"),
                    hi[:, par, h, :, :, 1:K + 1].bitcast(f32).rearrange("p n j k -> p (n j) k"),
                    ALU.subtract).then_inc(lo_done, 1)

            def w_lo(t, par):
                pool.wait_ge(whi_done, 4 * t + 4)
                nc.gpsimd.tensor_tensor(blocks(wlo, 0, par), wraw[:, par], blocks(whi, 0, par).bitcast(f32),
                                        ALU.subtract).then_inc(wlo_done, 1)

            def z_lo(tau, par):
                for h in range(2):
                    pool.wait_ge(zhi_done, 2 * tau + h + 1)
                    a, b = h * CH // 2, (h + 1) * CH // 2
                    nc.gpsimd.tensor_tensor(zlo[:, a:b], zin[:, par, a:b], zhi[:, a:b].bitcast(f32),
                                            ALU.subtract).then_inc(zlo_done, 1)

            def step(t, q, n, conv, mix, s, left):
                par = s % 2
                if mix and s:
                    z_lo(t - BLK, par)
                if conv and left:
                    w_lo(t + 1, 1 - par)
                    lo_half(t + 1, 1 - par, 0)
                    lo_half(t + 1, 1 - par, 1)
                if mix and not s:
                    z_lo(t - BLK, par)

            pool.wait_ge(pads_zeroed, 7)
            w_lo(0, 0)
            lo_half(0, 0, 0)
            lo_half(0, 0, 1)
            run(pool, step)

        @block_.scalar
        def _(act):
            act.wait_ge(consts_made, 8)
            nc.scalar.activation(gate[:, :], ones[:, :], ACT.Sigmoid).then_inc(gate_done, 1)

            def hi_half(t, par, h):
                act.wait_ge(xT_done, 4 * t + 2 * h + 2)
                need(act, conv_done, 4 * t + 2 * h - 6)
                nc.scalar.activation(hi[:, par, h, :, :, 1:K + 1].rearrange("p n j k -> p (n j) k"),
                                     xT[:, h].rearrange("p n j k -> p (n j) k"), ACT.Copy).then_inc(hi_done, 1)

            def w_hi(t, par):
                need(act, conv_done, 4 * t - 4)
                act.wait_ge(w_loaded[par], 16 * (t // 2) + 16)
                for g in range(GQ):
                    nc.scalar.activation(blocks(whi, g, par), wraw[:, par], ACT.Copy).then_inc(whi_done, 1)

            def pack(t, par, i):
                act.wait_ge(zt_done, 4 * t + i + 1)
                if i == 0:
                    need(act, z_stored[par], 16 * (t // 2))
                JW = (J - 1) * WO
                nc.scalar.activation(
                    zrow[:, par, i, :, 0:JW].rearrange("p h (j m) -> p h j m", m=WO),
                    zt[:, i % 2, :, 0:J - 1, 0:WO], ACT.Copy,
                    accum_out=sum_a[:, ds(t % (2 * BLK) * NC + i, 1)]).then_inc(zrow_done, 1)
                nc.scalar.activation(
                    zrow[:, par, i, :, JW:W], zt[:, i % 2, :, J - 1, 0:JT], ACT.Copy,
                    accum_out=sum_b[:, ds(t % (2 * BLK) * NC + i, 1)]).then_inc(zrow_done, 1)

            def z_hi(tau, par):
                act.wait_ge(z_loaded[par], 16 * (tau // 2) + 16)
                for h in range(2):
                    need(act, mix_done, 4 * tau - 2 + 2 * h)
                    a, b = h * CH // 2, (h + 1) * CH // 2
                    nc.scalar.activation(zhi[:, a:b], zin[:, par, a:b], ACT.Copy).then_inc(zhi_done, 1)

            def step(t, q, n, conv, mix, s, left):
                par = s % 2
                if mix and s:
                    z_hi(t - BLK, par)
                if conv:
                    if left:
                        w_hi(t + 1, 1 - par)
                    pack(t, par, 0)
                    if left:
                        hi_half(t + 1, 1 - par, 0)
                    pack(t, par, 1)
                    if left:
                        hi_half(t + 1, 1 - par, 1)
                    pack(t, par, 2)
                if mix and not s:
                    act.wait_ge(se_fc2, n + 1)
                    nc.scalar.activation(gate[:, :], ps_se[:, 2:3], ACT.Sigmoid,
                                         bias=vecd[:, 2:3]).then_inc(gate_done, 1)
                    act.wait_ge(w2_done, n + 1)
                    need(act, mix_done, 4 * (t - BLK))
                    nc.scalar.activation(w2hi[:, :], w2[:, :], ACT.Copy).then_inc(w2hi_done, 1)
                if conv:
                    pack(t, par, 3)
                if mix and not s:
                    z_hi(t - BLK, par)

            act.wait_ge(pads_zeroed, 7)
            w_hi(0, 0)
            hi_half(0, 0, 0)
            hi_half(0, 0, 1)
            run(act, step)

        @block_.vector
        def _(dve):
            for ap in (xin[:, :, :, :, 0:PAD].rearrange("p b n h w -> p (b n h) w"),
                       xin[:, :, :, :, PAD + W:XW].rearrange("p b n h w -> p (b n h) w"),
                       *(b[:, :, :, :, :, 0:K + 2:K + 1].bitcast(f32).rearrange("p a b n j k -> p (a b n j) k")
                         for b in (hi, lo)),
                       *(b[:, :, :, :, :].bitcast(f32).rearrange("p a c b m -> p (a c b m)") for b in (whi, wlo)),
                       w2[:, :]):
                nc.vector.memset(ap, 0.0).then_inc(pads_zeroed, 1)

            dve.wait_ge(kern_loaded, 3 * 16)
            dve.wait_ge(pads_zeroed, 7)
            nc.vector.tensor_tensor(k7[:, 1:6, 1:6], k7[:, 1:6, 1:6], k5[:, :, :], ALU.add).then_inc(kern_summed, 1)
            dve.wait_ge(kern_summed, 1)
            nc.vector.tensor_tensor(k7[:, 2:5, 2:5], k7[:, 2:5, 2:5], k3[:, :, :], ALU.add).then_inc(kern_summed, 1)
            dve.wait_ge(kern_summed, 2)
            dve.wait_ge(band_zeroed, 1)
            nc.vector.tensor_copy(band_taps, bass.AP(k7, 0, [[KS * KS, C], [0, WO], [1, KS], [KS, KS]])
                                  ).then_inc(band_made, 1)

            def patches(t, par, h):
                if h == 0:
                    dve.wait_ge(x_loaded[par], 64 * (t // 2) + 64)
                need(dve, hi_done, 2 * t + h - 1)
                need(dve, lo_done, 2 * t + h - 1)
                for kh in range(KH):
                    src = bass.AP(xin, (par * NC + 2 * h) * KH * XW + kh * XW,
                                  [[2 * NC * KH * XW, P], [KH * XW, 2], [WO, J], [1, B32]])
                    nc.vector.transpose(xT[:, h, :, :, kh * KK:kh * KK + KK], src).then_inc(xT_done, 1)

            def w_lo_copy(t, par):
                dve.wait_ge(wlo_done, t + 1)
                for g in range(1, GQ):
                    nc.vector.tensor_copy(blocks(wlo, g, par), blocks(wlo, 0, par).bitcast(f32)
                                          ).then_inc(wlo_copied, 1)

            patches(0, 0, 0)
            patches(0, 0, 1)

            dve.wait_ge(params_loaded, 9 * 16)
            nc.vector.tensor_tensor(vecs[:, 0:1], bdw[:, 0:1], bdw[:, 1:2], ALU.add).then_inc(bias_summed, 1)
            dve.wait_ge(bias_summed, 1)
            nc.vector.tensor_tensor(vecs[:, 0:1], vecs[:, 0:1], bdw[:, 2:3], ALU.add).then_inc(bias_summed, 1)
            dve.wait_ge(consts_made, 8)
            for h in range(KH):
                nc.vector.tensor_copy(w1d[:, :, h], w1s[:, :]).then_inc(bias_summed, 1)
            nc.vector.reduce_sum(half0[:, :], even[:, :], axis=mybir.AxisListType.X).then_inc(bias_summed, 1)
            dve.wait_ge(bias_summed, 5)
            nc.vector.tensor_scalar(half1[:, :], half0[:, :], -1.0, 1.0, ALU.mult, ALU.add).then_inc(bias_summed, 1)
            dve.wait_ge(bias_summed, 6)
            dve.wait_ge(small_mm, 4)
            nc.vector.tensor_copy(fc1T[:, 0:R], ps_se[0:C, 64:64 + R]).then_inc(small_copied, 1)
            nc.vector.tensor_copy(fc2T[:, :], ps_se[0:R, 128:256]).then_inc(small_copied, 1)
            nc.vector.tensor_copy(vecd[:, :], ps_se[:, 256:259]).then_inc(small_copied, 1)
            for h, halfh in enumerate((half0, half1)):
                nc.vector.tensor_scalar(wbase[:, :, h],
                                        ps_mix[:, 0, 0:P].rearrange("p (c h) -> p c h", h=KH)[:, :, h],
                                        halfh[:, 0:1], None, ALU.mult).then_inc(small_copied, 1)

            def rows(t, i):
                dve.wait_ge(conv_done, 4 * t + i + 1)
                need(dve, zrow_done, 2 * (4 * t + i - 1))
                nc.vector.transpose(zt[:, i % 2].rearrange("p h j m -> p h (j m)"),
                                    ps_conv[:, i % 2, :, 0:J * KK]).then_inc(zt_done, 1)

            def add(tau, par, i):
                if i == 0:
                    dve.wait_ge(res_loaded[par], 16 * (tau // 2) + 16)
                    need(dve, out_stored[par], 16 * (tau // 2))
                dve.wait_ge(mix_done, 4 * tau + i + 1)
                pick = lambda buf: buf[:, par].rearrange("p (k g w) -> p g k w", g=GQ, w=W)[:, GQ - 1 - i]
                nc.vector.scalar_tensor_tensor(
                    out=pick(oout), in0=ps_mix[:, i % 2, :].rearrange("p (k w) -> p k w", w=W),
                    scalar=obias[:, 0:1], in1=pick(xres), op0=ALU.add, op1=ALU.add).then_inc(out_done, 1)

            def step(t, q, n, conv, mix, s, left):
                par = s % 2
                head = mix and s == 0
                tau = t - BLK
                if head:
                    dve.wait_ge(zrow_done, 8 * t)
                    need(dve, se_sum, n)
                    nc.vector.tensor_tensor(cur[:, :], sum_a[:, ds(n % 2 * C, C)], sum_b[:, ds(n % 2 * C, C)],
                                            ALU.add).then_inc(cur_done, 1)
                if conv:
                    if left:
                        patches(t + 1, 1 - par, 0)
                    rows(t, 0)
                if head:
                    dve.wait_ge(se_sum, n + 1)
                    nc.vector.tensor_scalar(mean[:, :], ps_se[0:C, 0:1], 1.0 / (H * W), vecs[:, 0:1],
                                            ALU.mult, ALU.add).then_inc(mean_done, 1)
                if conv:
                    rows(t, 1)
                    if mix and not head:
                        add(tau, par, 0)
                if head:
                    dve.wait_ge(se_fc1, n + 1)
                    nc.vector.tensor_scalar(hid[:, :], ps_se[0:R, 1:2], fc1b[:, 0:1], 0.0,
                                            ALU.add, ALU.max).then_inc(hid_done, 1)
                if conv:
                    if left:
                        patches(t + 1, 1 - par, 1)
                    if left:
                        w_lo_copy(t + 1, 1 - par)
                    rows(t, 2)
                    if mix and not head:
                        add(tau, par, 1)
                if head:
                    dve.wait_ge(gate_done, n + 2)
                    need(dve, se_bias, n)
                    nc.vector.tensor_scalar(w2[:, :], wbase[:, :, :].rearrange("p c h -> p (c h)"), gate[:, 0:1],
                                            None, ALU.mult).then_inc(w2_done, 1)
                    dve.wait_ge(w2_done, n + 1)
                    dve.wait_ge(w2hi_done, n + 1)
                    nc.vector.tensor_tensor(w2lo[:, :], w2[:, :], w2hi[:, :].bitcast(f32),
                                            ALU.subtract).then_inc(w2lo_done, 1)
                if conv:
                    rows(t, 3)
                if head:
                    dve.wait_ge(se_bias, n + 1)
                    nc.vector.tensor_scalar(obias[:, :], ps_se[:, 3:4], vecd[:, 1:2], None,
                                            ALU.add).then_inc(obias_done, 1)
                    dve.wait_ge(obias_done, n + 1)
                if mix:
                    for i in range(2 if conv and not head else 0, 4):
                        add(tau, par, i)

            w_lo_copy(0, 0)
            run(dve, step)

        @block_.tensor
        def _(pe):
            mm = nc.tensor.matmul
            pe.wait_ge(bias_summed, 6)
            dupm = dup[:, :, :].rearrange("p c h -> p (c h)")
            for o, a, b in ((ps_se[0:C, 64:64 + R], fc1s[:, :], ident[0:R, 0:R]),
                            (ps_se[0:R, 128:256], fc2s[:, :], dupm),
                            (ps_se[:, 256:259], dupm, vecs[:, :]),
                            (ps_mix[:, 0, 0:P], w1d[:, :, :].rearrange("p c h -> p (c h)"), dupm)):
                mm(o, a, b, start=True, stop=True).then_inc(small_mm, 1)

            pe.wait_ge(small_copied, 5)
            def conv_chan(t, par, i):
                h, n = i // 2, i % 2
                if i == 0:
                    pe.wait_ge(wlo_copied, 3 * t + 3)
                if n == 0:
                    pe.wait_ge(lo_done, 2 * t + h + 1)
                need(pe, zt_done, 4 * t + i - 1)
                terms = [(w, src, dk) for dk in (1, 0, 2) for w, src in ((whi, hi), (whi, lo), (wlo, hi))]
                for m, (w, src, dk) in enumerate(terms):
                    for kh in range(KH):
                        last = mm(ps_conv[:, i % 2, kh, 0:J * KK], w[:, par, i, GQ * dk:GQ * dk + GQ].rearrange("p g m -> p (g m)"),
                                  src[:, par, h, n, :, kh * KK + dk:kh * KK + dk + KK],
                                  start=(m == 0), stop=(m == len(terms) - 1))
                last.then_inc(conv_done, 1)

            def mix_tile(tau, par, i):
                if i % 2 == 0:
                    pe.wait_ge(zlo_done, 2 * tau + i // 2 + 1)
                need(pe, out_done, 4 * tau + i - 1)
                a = i * TILE
                for m, (w, src) in enumerate(((w2hi, zhi), (w2hi, zlo), (w2lo, zhi))):
                    last = mm(ps_mix[:, i % 2, :], w[:, :], src[:, a:a + TILE], start=(m == 0), stop=(m == 2))
                last.then_inc(mix_done, 1)

            def step(t, q, n, conv, mix, s, left):
                par = s % 2
                tau = t - BLK
                if not (mix and s == 0):
                    order = ("c0", "c1", "m0", "c2", "m1", "c3", "m2", "m3")
                    for what in order:
                        i = int(what[1])
                        if what[0] == "c" and conv:
                            conv_chan(t, par, i)
                        if what[0] == "m" and mix:
                            mix_tile(tau, par, i)
                    return
                if conv:
                    conv_chan(t, par, 0)
                pe.wait_ge(cur_done, n + 1)
                mm(ps_se[0:C, 0:1], cur[:, :], ones[:, :], start=True, stop=True).then_inc(se_sum, 1)
                if conv:
                    conv_chan(t, par, 1)
                pe.wait_ge(mean_done, n + 1)
                mm(ps_se[:, 1:2], fc1T[:, :], mean[:, :], start=True, stop=True).then_inc(se_fc1, 1)
                if conv:
                    conv_chan(t, par, 2)
                pe.wait_ge(hid_done, n + 1)
                mm(ps_se[:, 2:3], fc2T[:, :], hid[:, :], start=True, stop=True).then_inc(se_fc2, 1)
                if conv:
                    conv_chan(t, par, 3)
                pe.wait_ge(w2_done, n + 1)
                mm(ps_se[:, 3:4], w2[:, :], vecd[:, 0:1], start=True, stop=True).then_inc(se_bias, 1)
                pe.wait_ge(w2lo_done, n + 1)
                for i in range(4):
                    mix_tile(tau, par, i)

            run(pe, step)


_INS = ["x", "L0_conv_w7", "L0_conv_b7", "L0_conv_w5", "L0_conv_b5", "L0_conv_w3", "L0_conv_b3", "L0_conv_fc1_w",
        "L0_conv_fc1_b", "L0_conv_fc2_w", "L0_conv_fc2_b", "L0_conv_w1x1", "L0_conv_b1x1"]


def kernel(**inputs):
    import numpy as _np
    import concourse.bacc as _bacc
    from concourse import mybir as _mybir
    from concourse.bass_utils import run_bass_kernel_spmd as _run

    nc = _bacc.Bacc("TRN2", target_bir_lowering=False, num_devices=1)
    arrays, args = {}, []
    for name in _INS:
        a = _np.ascontiguousarray(inputs[name])
        arrays[f"in_{name}_dram"] = a
        args.append(nc.dram_tensor(f"in_{name}_dram", a.shape, _mybir.dt.from_np(a.dtype), kind="ExternalInput").ap())
    shape = inputs["x"].shape
    args.append(nc.dram_tensor("out_0_dram", shape, _mybir.dt.float32, kind="ExternalOutput").ap())
    conv_se_kernel(nc, *args)
    r = _run(nc, [arrays], core_ids=[0])
    return r.results[0]["out_0_dram"]
```

```python
import concourse.bass as bass
from concourse import mybir
from contextlib import ExitStack


def conv_se_kernel(nc, x, w7, b7, w5, b5, w3, b3, fc1_w, fc1_b, fc2_w, fc2_b, w1x1, b1x1, out):
    f32 = mybir.dt.float32
    f32r = mybir.dt.float32r
    ALU = mybir.AluOpType
    ACT = mybir.ActivationFunctionType
    ds = bass.ds

    N, C, H, W = x.shape
    R = fc1_w.shape[0]
    KS = w7.shape[-1]
    PAD = KS // 2
    B32 = 32
    WO = B32 - (KS - 1)
    J = -(-W // WO)
    JT = W - (J - 1) * WO
    XW = (J - 1) * WO + B32
    GQ = 4
    KH = 2
    KK = H // GQ // KH
    K = KH * KK
    NC = 4
    DK = 3
    BANDS = DK * GQ
    HW2 = H * W // KH
    BLK = C // NC
    KKC = KK // BLK
    TILE = KKC * W
    CH = GQ * TILE
    P = 128
    STEPS = N * BLK

    zscr = nc.dram_tensor("z_scratch", (N, C, KH, GQ, KK, W), f32).ap()
    bscr = nc.dram_tensor("band_scratch", (C, B32, KS, WO), f32).ap()

    x_rows = x.rearrange("n c (h k g) w -> n g k (c h) w", h=KH, k=KK, g=GQ)
    z_rows = zscr.rearrange("n c h g k w -> n (g k) (c h) w")
    z_chan = zscr.rearrange("n c h g k w -> n (c h) g (k w)")
    b_steps = bscr.rearrange("(j r c) p a m -> j r p c (a m)", r=GQ, c=NC)
    x_chan = x.rearrange("n c (h r) w -> n (c h) (r w)", h=KH)
    out_chan = out.rearrange("n c (h r) w -> (n c h) (r w)", h=KH)

    ctx = ExitStack()
    with ctx:
        def sb(name, shape, dt=f32):
            return ctx.enter_context(nc.sbuf_tensor(name, shape, dt))

        def pb(name, shape):
            return ctx.enter_context(nc.psum_tensor(name, shape, f32))

        def sem(name):
            return ctx.enter_context(nc.semaphore(name))

        xin = sb("xin", [P, 2, NC, KH, XW])
        xT = sb("xT", [P, 2, 2, J, K])
        hi = sb("hi", [P, 2, 2, 2, J, K + 2], f32r)
        lo = sb("lo", [P, 2, 2, 2, J, K + 2], f32r)
        bands = sb("bands", [P, BLK // GQ, NC, KS, WO])
        whi = sb("whi", [P, 2, NC, BANDS, B32], f32r)
        wlo = sb("wlo", [P, 2, NC, BANDS, B32], f32r)
        zt = sb("zt", [P, 2, KH, J, B32])
        zrow = sb("zrow", [P, 2, NC, KH, W])
        sum_a = sb("sum_a", [P, 2 * C])
        sum_b = sb("sum_b", [P, 2 * C])
        mixbuf = sb("mixbuf", [P, 3, 2, CH])
        zin, xres, oout = mixbuf[:, 0], mixbuf[:, 1], mixbuf[:, 2]
        zhi = sb("zhi", [P, CH], f32r)
        zlo = sb("zlo", [P, CH], f32r)
        stage = bass.AP(mixbuf, 0, [[3 * 2 * CH, C], [1, B32 * KS * WO]])
        stage_taps = bass.AP(mixbuf, 0, [[3 * 2 * CH, C], [KS * WO + 1, WO], [KS * WO, KS], [WO, KS]])
        w2 = sb("w2", [P, P])
        w2hi = sb("w2hi", [P, P], f32r)
        w2lo = sb("w2lo", [P, P], f32r)
        obias = sb("obias", [P, 1])
        cur = sb("cur", [P, C])
        mean = sb("mean", [C, 1])
        hid = sb("hid", [R, 1])
        gate = sb("gate", [P, 1])
        ident = sb("ident", [C, C])
        dup = sb("dup", [C, C, KH])
        even = sb("even", [P, C])
        half0 = sb("half0", [P, 1])
        half1 = sb("half1", [P, 1])
        ones = sb("ones", [P, 1])
        k7 = sb("k7", [C, KS, KS])
        k5 = sb("k5", [C, 5, 5])
        k3 = sb("k3", [C, 3, 3])
        bdw = sb("bdw", [C, 3])
        vecs = sb("vecs", [C, 3])
        vecd = sb("vecd", [P, 3])
        fc1s = sb("fc1s", [R, C])
        fc1b = sb("fc1b", [R, 1])
        fc1T = sb("fc1T", [C, P])
        fc2s = sb("fc2s", [C, R])
        fc2T = sb("fc2T", [R, P])
        w1s = sb("w1s", [C, C])
        w1d = sb("w1d", [C, C, KH])
        wbase = sb("wbase", [P, C, KH])

        ps_conv = pb("ps_conv", [P, 2, KH, 512])
        ps_mix = pb("ps_mix", [P, 2, 512])
        ps_se = pb("ps_se", [P, 512])

        kern_loaded = sem("kern_loaded")
        params_loaded = sem("params_loaded")
        consts_made = sem("consts_made")
        pads_zeroed = sem("pads_zeroed")
        kern_summed = sem("kern_summed")
        bias_summed = sem("bias_summed")
        small_mm = sem("small_mm")
        small_copied = sem("small_copied")
        band_zeroed = sem("band_zeroed")
        band_made = sem("band_made")
        band_stored = [sem("band_stored0"), sem("band_stored1")]

        x_loaded = [sem("x_loaded0"), sem("x_loaded1")]
        bands_loaded = [sem("bands_loaded0"), sem("bands_loaded1")]
        xT_done = sem("xT_done")
        hi_done = sem("hi_done")
        lo_done = sem("lo_done")
        whi_done = sem("whi_done")
        wlo_done = sem("wlo_done")
        wlo_copied = sem("wlo_copied")
        conv_done = sem("conv_done")
        zt_done = sem("zt_done")
        zrow_done = sem("zrow_done")
        z_stored = [sem("z_stored0"), sem("z_stored1")]

        z_loaded = [sem("z_loaded0"), sem("z_loaded1")]
        z_tail_loaded = sem("z_tail_loaded")
        res_loaded = [sem("res_loaded0"), sem("res_loaded1")]
        zhi_done = sem("zhi_done")
        zlo_done = sem("zlo_done")
        mix_done = sem("mix_done")
        out_done = sem("out_done")
        out_stored = [sem("out_stored0"), sem("out_stored1")]

        cur_done = sem("cur_done")
        se_sum = sem("se_sum")
        mean_done = sem("mean_done")
        se_fc1 = sem("se_fc1")
        hid_done = sem("hid_done")
        se_fc2 = sem("se_fc2")
        gate_done = sem("gate_done")
        w2_done = sem("w2_done")
        w2hi_done = sem("w2hi_done")
        w2lo_done = sem("w2lo_done")
        se_bias = sem("se_bias")
        obias_done = sem("obias_done")

        def need(eng, s, v):
            if not isinstance(v, int) or v > 0:
                eng.wait_ge(s, v)

        def run(engine, step):
            def block(b, conv, first=False, last=False):
                step(b * BLK, 0, b - 1, conv, True, 0, 2)
                if first:
                    for q in range(1, 5):
                        step(b * BLK + q, q, b - 1, conv, True, q, 2)
                with engine.Fori(1 if first else 0, BLK // 4 - 1) as quad:
                    for s in range(1, 5):
                        q = 4 * quad + s
                        step(b * BLK + q, q, b - 1, conv, True, s, 2)
                step(b * BLK + BLK - 3, BLK - 3, b - 1, conv, True, 1, 2)
                step(b * BLK + BLK - 2, BLK - 2, b - 1, conv, True, 2, 1 if last else 2)
                step(b * BLK + BLK - 1, BLK - 1, b - 1, conv, True, BLK - 1, 0 if last else 2)

            for q in range(4):
                step(q, q, -1, True, False, q, 2)
            with engine.Fori(1, BLK // 4 - 1) as quad:
                for s in range(4, 8):
                    q = 4 * quad + s - 4
                    step(q, q, -1, True, False, s, 2)
            for q, s in ((BLK - 4, 4), (BLK - 3, 1), (BLK - 2, 2), (BLK - 1, BLK - 1)):
                step(q, q, -1, True, False, s, 2)
            block(1, True, first=True)
            with engine.Fori(2, N - 1) as b:
                block(b, True)
            block(N - 1, True, last=True)
            block(N, False)

        def blocks(w, g, par):
            return w[B32 * g:B32 * g + B32, par, :, GQ - g:GQ - g + KS, 0:WO]

        def wait_bands(eng, t):
            if isinstance(t, int) and t in (0, GQ):
                eng.wait_ge(bands_loaded[t // GQ], 16 * (GQ if t == 0 else BLK - GQ))

        block_ = ctx.enter_context(nc.Block())

        @block_.sync
        def _(sp):
            col = lambda v: v.rearrange("(c a) -> c a", a=1)
            for dst, src in ((k7[:, :, :], w7[:, 0]), (k5[:, :, :], w5[:, 0]), (k3[:, :, :], w3[:, 0])):
                sp.dma_start(dst, src).then_inc(kern_loaded, 16)

            def load_x(n, q, par):
                for g in (0, 2, 1, 3):
                    sp.dma_start(xin[B32 * g:B32 * g + B32, par, :, :, PAD:PAD + W].rearrange("p c h w -> p (c h) w"),
                                 x_rows[n, g, :, ds(q * NC * KH, NC * KH), :]
                                 ).then_inc(x_loaded[par], 16)

            load_x(0, 0, 0)
            for dst, src in ((bdw[:, 0:1], col(b7)), (bdw[:, 1:2], col(b5)), (bdw[:, 2:3], col(b3)),
                             (vecs[:, 1:2], col(b1x1)), (vecs[:, 2:3], col(fc2_b)),
                             (fc1s[:, :], fc1_w), (fc1b[:, :], col(fc1_b)), (fc2s[:, :], fc2_w),
                             (w1s[:, :], w1x1[:, :, 0, 0])):
                sp.dma_start(dst, src).then_inc(params_loaded, 16)
            sp.wait_ge(band_made, 1)
            FIRST = GQ * NC
            for part, (c0, c1) in enumerate(((0, FIRST), (FIRST, C))):
                sp.dma_start(bscr[c0:c1].rearrange("c p a m -> c (p a m)"), stage[c0:c1]
                             ).then_inc(band_stored[part], 16)
            for j in range(BLK // GQ):
                if j < 2:
                    sp.wait_ge(band_stored[j], 16)
                for r in range(GQ):
                    sp.dma_start(bands[B32 * r:B32 * r + B32, j].rearrange("p c a m -> p c (a m)"), b_steps[j, r]
                                 ).then_inc(bands_loaded[min(j, 1)], 16)
                if j == 0:
                    load_x(0, 1, 1)

            TAIL = (C - NC) * KH

            def store_out(n, q, par):
                sp.dma_start(out_chan[ds(n * P, P), ds(q * CH, CH)], oout[:, par]).then_inc(out_stored[par], 16)

            def load_z(n, s, par, p1=P):
                sp.dma_start(zin[0:p1, par].rearrange("p (g a) -> p g a", g=GQ),
                             z_chan[n, 0:p1, :, ds(s * TILE, TILE)]).then_inc(z_loaded[par], 16)

            def load_res(n, s, par):
                sp.dma_start(xres[:, par], x_chan[n, :, ds(s * CH, CH)]).then_inc(res_loaded[par], 16)

            def step(t, q, n, conv, mix, s, left):
                par = s % 2
                tau = t - BLK
                if mix and 0 < s < BLK - 1:
                    sp.wait_ge(zlo_done, 2 * tau)
                    load_z(n, q + 1, 1 - par)
                if conv and left == 2:
                    sp.wait_ge(xT_done, 4 * t + 4)
                    load_x((t + 2) // BLK, (t + 2) % BLK, par)
                if mix and s == 0:
                    sp.wait_ge(z_stored[1], 16 * (t // 2))
                    sp.dma_start(zin[TAIL:P, 0].rearrange("p (g a) -> p g a", g=GQ),
                                 z_chan[n, TAIL:P, :, 0:TILE]).then_inc(z_tail_loaded, 16)
                    need(sp, zlo_done, 2 * tau)
                    load_z(n, 1, 1)
                if mix:
                    if not (isinstance(t, int) and t == BLK):
                        sp.wait_ge(out_done, 4 * tau)
                        store_out(n if s else n - 1, q - 1 if s else BLK - 1, 1 - par)
                    if s < BLK - 1:
                        load_res(n, q + 1, 1 - par)
                if conv and s == BLK - 1:
                    sp.wait_ge(z_stored[1], 16 * (t // 2))
                    load_res(n + 1, 0, 0)
                    sp.wait_ge(z_stored[0], 16 * (t // 2 + 1))
                    load_z(n + 1, 0, 0, TAIL)
                if conv:
                    sp.wait_ge(zrow_done, 8 * t + 8)
                    sp.dma_start(z_rows[n + 1, :, ds(q * NC * KH, NC * KH), :],
                                 zrow[:, par].rearrange("p c h w -> p (c h) w")).then_inc(z_stored[par], 16)

            run(sp, step)
            sp.wait_ge(out_done, 4 * N * BLK)
            store_out(N - 1, BLK - 1, 1)
            sp.wait_ge(out_stored[0], 16 * N * BLK // 2)
            sp.wait_ge(out_stored[1], 16 * N * BLK // 2)

        @block_.gpsimd
        def _(pool):
            def zero(ap):
                nc.gpsimd.memset(ap, 0.0).then_inc(consts_made, 1)

            nc.gpsimd.memset(stage, 0.0).then_inc(band_zeroed, 1)
            zero(ident[:, :])
            zero(dup[:, :, :])
            zero(even[:, :])
            zero(fc1T[:, :])
            nc.gpsimd.memset(ones[:, :], 1.0).then_inc(consts_made, 1)
            pool.wait_ge(consts_made, 5)
            for ap, pattern, cm in ((ident[:, :], [[-1, C]], 1), (dup[:, :, :], [[-1, C], [0, KH]], 1),
                                    (even[:, :], [[-2, C]], 1)):
                nc.gpsimd.affine_select(out=ap, in_=ap, compare_op=ALU.not_equal, fill=1.0, base=0,
                                        pattern=pattern, channel_multiplier=cm).then_inc(consts_made, 1)

            def lo_half(t, par, h):
                pool.wait_ge(hi_done, 2 * t + h + 1)
                nc.gpsimd.tensor_tensor(
                    lo[:, par, h, :, :, 1:K + 1].rearrange("p n j k -> p (n j) k"),
                    xT[:, h].rearrange("p n j k -> p (n j) k"),
                    hi[:, par, h, :, :, 1:K + 1].bitcast(f32).rearrange("p n j k -> p (n j) k"),
                    ALU.subtract).then_inc(lo_done, 1)

            def z_lo(tau, par):
                for h in range(2):
                    pool.wait_ge(zhi_done, 2 * tau + h + 1)
                    a, b = h * CH // 2, (h + 1) * CH // 2
                    nc.gpsimd.tensor_tensor(zlo[:, a:b], zin[:, par, a:b], zhi[:, a:b].bitcast(f32),
                                            ALU.subtract).then_inc(zlo_done, 1)

            def step(t, q, n, conv, mix, s, left):
                par = s % 2
                if mix and s:
                    z_lo(t - BLK, par)
                if conv and left:
                    lo_half(t + 1, 1 - par, 0)
                    lo_half(t + 1, 1 - par, 1)
                if mix and not s:
                    z_lo(t - BLK, par)

            pool.wait_ge(pads_zeroed, 7)
            lo_half(0, 0, 0)
            lo_half(0, 0, 1)
            run(pool, step)

        @block_.scalar
        def _(act):
            act.wait_ge(consts_made, 8)
            nc.scalar.activation(gate[:, :], ones[:, :], ACT.Sigmoid).then_inc(gate_done, 1)

            def hi_half(t, par, h):
                act.wait_ge(xT_done, 4 * t + 2 * h + 2)
                need(act, conv_done, 4 * t + 2 * h - 6)
                nc.scalar.activation(hi[:, par, h, :, :, 1:K + 1].rearrange("p n j k -> p (n j) k"),
                                     xT[:, h].rearrange("p n j k -> p (n j) k"), ACT.Copy).then_inc(hi_done, 1)

            def w_hi(t, q, s):
                wait_bands(act, t)
                need(act, conv_done, 4 * t - 4)
                r = s % GQ
                for g in range(GQ):
                    nc.scalar.activation(blocks(whi, g, s % 2), bands[B32 * r:B32 * r + B32, q // GQ], ACT.Copy
                                         ).then_inc(whi_done, 1)

            def pack(t, par, i):
                act.wait_ge(zt_done, 4 * t + i + 1)
                if i == 0:
                    need(act, z_stored[par], 16 * (t // 2))
                JW = (J - 1) * WO
                nc.scalar.activation(
                    zrow[:, par, i, :, 0:JW].rearrange("p h (j m) -> p h j m", m=WO),
                    zt[:, i % 2, :, 0:J - 1, 0:WO], ACT.Copy,
                    accum_out=sum_a[:, ds(t % (2 * BLK) * NC + i, 1)]).then_inc(zrow_done, 1)
                nc.scalar.activation(
                    zrow[:, par, i, :, JW:W], zt[:, i % 2, :, J - 1, 0:JT], ACT.Copy,
                    accum_out=sum_b[:, ds(t % (2 * BLK) * NC + i, 1)]).then_inc(zrow_done, 1)

            def z_hi(tau, par, n, head):
                act.wait_ge(z_loaded[par], 16 * (tau // 2) + 16)
                if head:
                    act.wait_ge(z_tail_loaded, 16 * n + 16)
                for h in range(2):
                    need(act, mix_done, 4 * tau - 2 + 2 * h)
                    a, b = h * CH // 2, (h + 1) * CH // 2
                    nc.scalar.activation(zhi[:, a:b], zin[:, par, a:b], ACT.Copy).then_inc(zhi_done, 1)

            def step(t, q, n, conv, mix, s, left):
                par = s % 2
                if mix and s:
                    z_hi(t - BLK, par, n, s == 0)
                if conv:
                    if left:
                        w_hi(t + 1, (q + 1) % BLK, s + 1)
                    pack(t, par, 0)
                    if left:
                        hi_half(t + 1, 1 - par, 0)
                    pack(t, par, 1)
                    if left:
                        hi_half(t + 1, 1 - par, 1)
                    pack(t, par, 2)
                if mix and not s:
                    act.wait_ge(se_fc2, n + 1)
                    nc.scalar.activation(gate[:, :], ps_se[:, 2:3], ACT.Sigmoid,
                                         bias=vecd[:, 2:3]).then_inc(gate_done, 1)
                    act.wait_ge(w2_done, n + 1)
                    need(act, mix_done, 4 * (t - BLK))
                    nc.scalar.activation(w2hi[:, :], w2[:, :], ACT.Copy).then_inc(w2hi_done, 1)
                    z_hi(t - BLK, par, n, s == 0)
                if conv:
                    pack(t, par, 3)

            act.wait_ge(pads_zeroed, 7)
            w_hi(0, 0, 0)
            hi_half(0, 0, 0)
            hi_half(0, 0, 1)
            run(act, step)

        @block_.vector
        def _(dve):
            dve.wait_ge(kern_loaded, 3 * 16)
            nc.vector.tensor_tensor(k7[:, 1:6, 1:6], k7[:, 1:6, 1:6], k5[:, :, :], ALU.add).then_inc(kern_summed, 1)
            dve.wait_ge(kern_summed, 1)
            nc.vector.tensor_tensor(k7[:, 2:5, 2:5], k7[:, 2:5, 2:5], k3[:, :, :], ALU.add).then_inc(kern_summed, 1)
            dve.wait_ge(kern_summed, 2)
            dve.wait_ge(band_zeroed, 1)
            nc.vector.tensor_copy(stage_taps, bass.AP(k7, 0, [[KS * KS, C], [0, WO], [1, KS], [KS, KS]])
                                  ).then_inc(band_made, 1)

            for ap in (xin[:, :, :, :, 0:PAD].rearrange("p b n h w -> p (b n h) w"),
                       xin[:, :, :, :, PAD + W:XW].rearrange("p b n h w -> p (b n h) w"),
                       *(b[:, :, :, :, :, 0:K + 2:K + 1].bitcast(f32).rearrange("p a b n j k -> p (a b n j) k")
                         for b in (hi, lo)),
                       *(b[:, :, :, :, :].bitcast(f32).rearrange("p a c b m -> p (a c b m)") for b in (whi, wlo)),
                       w2[:, :]):
                nc.vector.memset(ap, 0.0).then_inc(pads_zeroed, 1)
            dve.wait_ge(pads_zeroed, 7)

            def patches(t, par, h):
                if h == 0:
                    dve.wait_ge(x_loaded[par], 64 * (t // 2) + 64)
                need(dve, hi_done, 2 * t + h - 1)
                need(dve, lo_done, 2 * t + h - 1)
                for kh in range(KH):
                    src = bass.AP(xin, (par * NC + 2 * h) * KH * XW + kh * XW,
                                  [[2 * NC * KH * XW, P], [KH * XW, 2], [WO, J], [1, B32]])
                    nc.vector.transpose(xT[:, h, :, :, kh * KK:kh * KK + KK], src).then_inc(xT_done, 1)

            def w_lo(t, q, s):
                wait_bands(dve, t)
                dve.wait_ge(whi_done, 4 * t + 4)
                need(dve, conv_done, 4 * t - 4)
                r, par = s % GQ, s % 2
                nc.vector.tensor_tensor(blocks(wlo, r, par), bands[B32 * r:B32 * r + B32, q // GQ],
                                        blocks(whi, r, par).bitcast(f32), ALU.subtract).then_inc(wlo_done, 1)
                dve.wait_ge(wlo_done, t + 1)
                for g in range(GQ):
                    if g != r:
                        nc.vector.tensor_copy(blocks(wlo, g, par), blocks(wlo, r, par).bitcast(f32)
                                              ).then_inc(wlo_copied, 1)

            patches(0, 0, 0)
            patches(0, 0, 1)

            dve.wait_ge(params_loaded, 9 * 16)
            nc.vector.tensor_tensor(vecs[:, 0:1], bdw[:, 0:1], bdw[:, 1:2], ALU.add).then_inc(bias_summed, 1)
            dve.wait_ge(bias_summed, 1)
            nc.vector.tensor_tensor(vecs[:, 0:1], vecs[:, 0:1], bdw[:, 2:3], ALU.add).then_inc(bias_summed, 1)
            dve.wait_ge(consts_made, 8)
            for h in range(KH):
                nc.vector.tensor_copy(w1d[:, :, h], w1s[:, :]).then_inc(bias_summed, 1)
            nc.vector.reduce_sum(half0[:, :], even[:, :], axis=mybir.AxisListType.X).then_inc(bias_summed, 1)
            dve.wait_ge(bias_summed, 5)
            nc.vector.tensor_scalar(half1[:, :], half0[:, :], -1.0, 1.0, ALU.mult, ALU.add).then_inc(bias_summed, 1)
            dve.wait_ge(bias_summed, 6)
            dve.wait_ge(small_mm, 4)
            nc.vector.tensor_copy(fc1T[:, 0:R], ps_se[0:C, 64:64 + R]).then_inc(small_copied, 1)
            nc.vector.tensor_copy(fc2T[:, :], ps_se[0:R, 128:256]).then_inc(small_copied, 1)
            nc.vector.tensor_copy(vecd[:, :], ps_se[:, 256:259]).then_inc(small_copied, 1)
            for h, halfh in enumerate((half0, half1)):
                nc.vector.tensor_scalar(wbase[:, :, h],
                                        ps_mix[:, 0, 0:P].rearrange("p (c h) -> p c h", h=KH)[:, :, h],
                                        halfh[:, 0:1], None, ALU.mult).then_inc(small_copied, 1)

            def rows(t, i):
                dve.wait_ge(conv_done, 4 * t + i + 1)
                need(dve, zrow_done, 2 * (4 * t + i - 1))
                nc.vector.transpose(zt[:, i % 2].rearrange("p h j m -> p h (j m)"),
                                    ps_conv[:, i % 2, :, 0:J * KK]).then_inc(zt_done, 1)

            def add(tau, par, i):
                if i == 0:
                    dve.wait_ge(res_loaded[par], 16 * (tau // 2) + 16)
                    need(dve, out_stored[par], 16 * (tau // 2))
                dve.wait_ge(mix_done, 4 * tau + i + 1)
                pick = lambda buf: buf[:, par].rearrange("p (k g w) -> p g k w", g=GQ, w=W)[:, GQ - 1 - i]
                nc.vector.scalar_tensor_tensor(
                    out=pick(oout), in0=ps_mix[:, i % 2, :].rearrange("p (k w) -> p k w", w=W),
                    scalar=obias[:, 0:1], in1=pick(xres), op0=ALU.add, op1=ALU.add).then_inc(out_done, 1)

            def step(t, q, n, conv, mix, s, left):
                par = s % 2
                head = mix and s == 0
                tau = t - BLK
                if head:
                    dve.wait_ge(zrow_done, 8 * t)
                    need(dve, se_sum, n)
                    nc.vector.tensor_tensor(cur[:, :], sum_a[:, ds(n % 2 * C, C)], sum_b[:, ds(n % 2 * C, C)],
                                            ALU.add).then_inc(cur_done, 1)
                if conv:
                    if left:
                        patches(t + 1, 1 - par, 0)
                    rows(t, 0)
                if head:
                    dve.wait_ge(se_sum, n + 1)
                    nc.vector.tensor_scalar(mean[:, :], ps_se[0:C, 0:1], 1.0 / (H * W), vecs[:, 0:1],
                                            ALU.mult, ALU.add).then_inc(mean_done, 1)
                if conv:
                    rows(t, 1)
                    if mix and not head:
                        add(tau, par, 0)
                if head:
                    dve.wait_ge(se_fc1, n + 1)
                    nc.vector.tensor_scalar(hid[:, :], ps_se[0:R, 1:2], fc1b[:, 0:1], 0.0,
                                            ALU.add, ALU.max).then_inc(hid_done, 1)
                if conv:
                    if left:
                        patches(t + 1, 1 - par, 1)
                    if left:
                        w_lo(t + 1, (q + 1) % BLK, s + 1)
                    rows(t, 2)
                    if mix and not head:
                        add(tau, par, 1)
                if head:
                    dve.wait_ge(gate_done, n + 2)
                    need(dve, se_bias, n)
                    nc.vector.tensor_scalar(w2[:, :], wbase[:, :, :].rearrange("p c h -> p (c h)"), gate[:, 0:1],
                                            None, ALU.mult).then_inc(w2_done, 1)
                    dve.wait_ge(w2_done, n + 1)
                    dve.wait_ge(w2hi_done, n + 1)
                    nc.vector.tensor_tensor(w2lo[:, :], w2[:, :], w2hi[:, :].bitcast(f32),
                                            ALU.subtract).then_inc(w2lo_done, 1)
                if conv:
                    rows(t, 3)
                if head:
                    dve.wait_ge(se_bias, n + 1)
                    nc.vector.tensor_scalar(obias[:, :], ps_se[:, 3:4], vecd[:, 1:2], None,
                                            ALU.add).then_inc(obias_done, 1)
                    dve.wait_ge(obias_done, n + 1)
                if mix:
                    for i in range(2 if conv and not head else 0, 4):
                        add(tau, par, i)

            w_lo(0, 0, 0)
            run(dve, step)

        @block_.tensor
        def _(pe):
            mm = nc.tensor.matmul
            pe.wait_ge(bias_summed, 6)
            dupm = dup[:, :, :].rearrange("p c h -> p (c h)")
            for o, a, b in ((ps_se[0:C, 64:64 + R], fc1s[:, :], ident[0:R, 0:R]),
                            (ps_se[0:R, 128:256], fc2s[:, :], dupm),
                            (ps_se[:, 256:259], dupm, vecs[:, :]),
                            (ps_mix[:, 0, 0:P], w1d[:, :, :].rearrange("p c h -> p (c h)"), dupm)):
                mm(o, a, b, start=True, stop=True).then_inc(small_mm, 1)

            pe.wait_ge(small_copied, 5)
            def conv_chan(t, par, i):
                h, n = i // 2, i % 2
                if i == 0:
                    pe.wait_ge(wlo_copied, 3 * t + 3)
                if n == 0:
                    pe.wait_ge(lo_done, 2 * t + h + 1)
                need(pe, zt_done, 4 * t + i - 1)
                terms = [(w, src, dk) for dk in (1, 0, 2) for w, src in ((whi, hi), (whi, lo), (wlo, hi))]
                for m, (w, src, dk) in enumerate(terms):
                    for kh in range(KH):
                        last = mm(ps_conv[:, i % 2, kh, 0:J * KK], w[:, par, i, GQ * dk:GQ * dk + GQ].rearrange("p g m -> p (g m)"),
                                  src[:, par, h, n, :, kh * KK + dk:kh * KK + dk + KK],
                                  start=(m == 0), stop=(m == len(terms) - 1))
                last.then_inc(conv_done, 1)

            def mix_tile(tau, par, i):
                if i % 2 == 0:
                    pe.wait_ge(zlo_done, 2 * tau + i // 2 + 1)
                need(pe, out_done, 4 * tau + i - 1)
                a = i * TILE
                for m, (w, src) in enumerate(((w2hi, zhi), (w2hi, zlo), (w2lo, zhi))):
                    last = mm(ps_mix[:, i % 2, :], w[:, :], src[:, a:a + TILE], start=(m == 0), stop=(m == 2))
                last.then_inc(mix_done, 1)

            def step(t, q, n, conv, mix, s, left):
                par = s % 2
                tau = t - BLK
                if not (mix and s == 0):
                    order = ("c0", "c1", "m0", "c2", "m1", "c3", "m2", "m3")
                    for what in order:
                        i = int(what[1])
                        if what[0] == "c" and conv:
                            conv_chan(t, par, i)
                        if what[0] == "m" and mix:
                            mix_tile(tau, par, i)
                    return
                if conv:
                    conv_chan(t, par, 0)
                pe.wait_ge(cur_done, n + 1)
                mm(ps_se[0:C, 0:1], cur[:, :], ones[:, :], start=True, stop=True).then_inc(se_sum, 1)
                if conv:
                    conv_chan(t, par, 1)
                pe.wait_ge(mean_done, n + 1)
                mm(ps_se[:, 1:2], fc1T[:, :], mean[:, :], start=True, stop=True).then_inc(se_fc1, 1)
                if conv:
                    conv_chan(t, par, 2)
                pe.wait_ge(hid_done, n + 1)
                mm(ps_se[:, 2:3], fc2T[:, :], hid[:, :], start=True, stop=True).then_inc(se_fc2, 1)
                if conv:
                    conv_chan(t, par, 3)
                pe.wait_ge(w2_done, n + 1)
                mm(ps_se[:, 3:4], w2[:, :], vecd[:, 0:1], start=True, stop=True).then_inc(se_bias, 1)
                pe.wait_ge(w2lo_done, n + 1)
                for i in range(4):
                    mix_tile(tau, par, i)

            run(pe, step)


_INS = ["x", "L0_conv_w7", "L0_conv_b7", "L0_conv_w5", "L0_conv_b5", "L0_conv_w3", "L0_conv_b3", "L0_conv_fc1_w",
        "L0_conv_fc1_b", "L0_conv_fc2_w", "L0_conv_fc2_b", "L0_conv_w1x1", "L0_conv_b1x1"]


def kernel(**inputs):
    import numpy as _np
    import concourse.bacc as _bacc
    from concourse import mybir as _mybir
    from concourse.bass_utils import run_bass_kernel_spmd as _run

    nc = _bacc.Bacc("TRN2", target_bir_lowering=False, num_devices=1)
    arrays, args = {}, []
    for name in _INS:
        a = _np.ascontiguousarray(inputs[name])
        arrays[f"in_{name}_dram"] = a
        args.append(nc.dram_tensor(f"in_{name}_dram", a.shape, _mybir.dt.from_np(a.dtype), kind="ExternalInput").ap())
    shape = inputs["x"].shape
    args.append(nc.dram_tensor("out_0_dram", shape, _mybir.dt.float32, kind="ExternalOutput").ap())
    conv_se_kernel(nc, *args)
    r = _run(nc, [arrays], core_ids=[0])
    return r.results[0]["out_0_dram"]
```
